# Optimizing a Trainium2 kernel written in Bass

```python
import numpy as np
import jax
import jax.numpy as jnp

def _softmax(x, axis=-1):
    return jax.nn.softmax(x, axis=axis)

def _gelu(x):
    return jax.nn.gelu(x, approximate=True)

def _silu(x):
    return jax.nn.silu(x)

def _sigmoid(x):
    return jax.nn.sigmoid(x)

def _layernorm(x, axis=-1, eps=1e-05):
    m = jnp.mean(x, axis=axis, keepdims=True)
    v = jnp.var(x, axis=axis, keepdims=True)
    return (x - m) / jnp.sqrt(v + eps)

def _scatter_add(tgt, idx, src, axis=0):
    return tgt.at[idx].add(src)

def _segment_sum(src, seg, n):
    return jax.ops.segment_sum(src, seg, n)
kernel_name = 'mk_sandwich_d1_jaxref_r8_79b922'

def setup_inputs(seed: int=0):
    np.random.seed(seed)
    _w = jnp.asarray

    def _L0_attn_setup():
        import math
        import jax, jax.numpy as jnp
        import numpy as np
        NUM_HEADS = 16
        EMBED = 128
        B, T = (2, 256)
        key = jax.random.key(seed)
        k1, k2 = jax.random.split(key)
        x = jax.random.normal(k1, (B, T, EMBED), dtype=jnp.float32)
        bound = 1.0 / math.sqrt(NUM_HEADS * EMBED)
        weight = jax.random.uniform(k2, (NUM_HEADS * EMBED, EMBED), dtype=jnp.float32, minval=-bound, maxval=bound)
        return {'x': x, 'weight': weight}
    _L0_attn_in = _L0_attn_setup()

    def _L0_ffn_setup():
        import jax, jax.numpy as jnp
        import numpy as np
        DIM = 128

        def _reference_tuple_inner(x, W_r, W_k, W_v, mu_r, mu_k):
            B, T, C = x.shape
            x_prev = jnp.concatenate([jnp.zeros((B, 1, C), x.dtype), x[:, :-1, :]], axis=1)
            xr = mu_r * x + (1.0 - mu_r) * x_prev
            xk = mu_k * x + (1.0 - mu_k) * x_prev
            r = jax.nn.sigmoid(jnp.einsum('btc,dc->btd', xr, W_r))
            k = jnp.einsum('btc,dc->btd', xk, W_k)
            k_act = jnp.square(jax.nn.relu(k))
            out = r * jnp.einsum('btc,dc->btd', k_act, W_v)
            new_state = x[:, -1, :]
            return (out, new_state)
        key = jax.random.key(seed)
        ks = jax.random.split(key, 6)
        B, T, C = (8, 256, DIM)
        x = jax.random.normal(ks[0], (B, T, C), dtype=jnp.float32)
        s = 1.0 / np.sqrt(C)
        W_r = jax.random.uniform(ks[1], (C, C), jnp.float32, -s, s)
        W_k = jax.random.uniform(ks[2], (C, C), jnp.float32, -s, s)
        W_v = jax.random.uniform(ks[3], (C, C), jnp.float32, -s, s)
        mu_r = jax.random.uniform(ks[4], (C,), jnp.float32)
        mu_k = jax.random.uniform(ks[5], (C,), jnp.float32)
        return {'x': x, 'W_r': W_r, 'W_k': W_k, 'W_v': W_v, 'mu_r': mu_r, 'mu_k': mu_k}
    _L0_ffn_in = _L0_ffn_setup()
    _d = {'L0_attn_x': _L0_attn_in['x'], 'L0_attn_weight': _L0_attn_in['weight'], 'L0_ffn_W_r': _L0_ffn_in['W_r'], 'L0_ffn_W_k': _L0_ffn_in['W_k'], 'L0_ffn_W_v': _L0_ffn_in['W_v'], 'L0_ffn_mu_r': _L0_ffn_in['mu_r'], 'L0_ffn_mu_k': _L0_ffn_in['mu_k']}
    _x0 = _d['L0_attn_x']
    _d['L0_attn_x'] = jax.random.normal(jax.random.fold_in(jax.random.key(seed), 1), (4, 1024, 128), dtype=_x0.dtype)
    del _x0
    return _d

def reference(L0_attn_x, L0_attn_weight, L0_ffn_W_r, L0_ffn_W_k, L0_ffn_W_v, L0_ffn_mu_r, L0_ffn_mu_k):

    def _L0_attn_ref(x, weight):
        import math
        import jax, jax.numpy as jnp
        import numpy as np
        NUM_HEADS = 16
        EMBED = 128
        B, T = (2, 256)
        b, t, c = x.shape
        nh = NUM_HEADS
        hs = c // nh
        y = x.reshape(b, t, nh, hs).transpose(0, 2, 1, 3)
        scores = jnp.einsum('bhtk,bhsk->bhts', y, y) / math.sqrt(hs)
        attn = jax.nn.softmax(scores, axis=-1)
        o = jnp.einsum('bhts,bsc->bhtc', attn, x)
        o = o.transpose(0, 2, 1, 3).reshape(b, t, nh * c)
        return o @ weight

    def _L0_ffn_ref(x, W_r, W_k, W_v, mu_r, mu_k):
        import jax, jax.numpy as jnp
        import numpy as np
        DIM = 128

        def _reference_tuple_inner(x, W_r, W_k, W_v, mu_r, mu_k):
            B, T, C = x.shape
            x_prev = jnp.concatenate([jnp.zeros((B, 1, C), x.dtype), x[:, :-1, :]], axis=1)
            xr = mu_r * x + (1.0 - mu_r) * x_prev
            xk = mu_k * x + (1.0 - mu_k) * x_prev
            r = jax.nn.sigmoid(jnp.einsum('btc,dc->btd', xr, W_r))
            k = jnp.einsum('btc,dc->btd', xk, W_k)
            k_act = jnp.square(jax.nn.relu(k))
            out = r * jnp.einsum('btc,dc->btd', k_act, W_v)
            new_state = x[:, -1, :]
            return (out, new_state)
        return _reference_tuple_inner(x, W_r, W_k, W_v, mu_r, mu_k)[0]
    x = L0_attn_x
    x = x + _layernorm(_L0_attn_ref(_layernorm(x, axis=-1), L0_attn_weight), axis=-1)
    x = x + _layernorm(_L0_ffn_ref(_layernorm(x, axis=-1), L0_ffn_W_r, L0_ffn_W_k, L0_ffn_W_v, L0_ffn_mu_r, L0_ffn_mu_k), axis=-1)
    return x

_drawn_inputs = setup_inputs


def setup_inputs(seed=0):
    import zlib

    import numpy as np

    out = dict(_drawn_inputs(seed))
    spreads = {}
    factors = {}
    for name, (base, spread) in spreads.items():
        noise = np.random.default_rng([zlib.crc32(name.encode()), seed]).standard_normal(out[name].shape)
        drawn = base * np.exp(spread * noise) if base else spread * noise
        out[name] = jnp.asarray(drawn.astype(out[name].dtype))
    for name, factor in factors.items():
        out[name] = (out[name] * factor).astype(out[name].dtype)
    return out
```

```python
from contextlib import ExitStack

import concourse.bass as bass
from concourse import mybir

F32 = mybir.dt.float32
F16 = mybir.dt.float16
I32 = mybir.dt.int32
ALU = mybir.AluOpType
ACT = mybir.ActivationFunctionType
AX = mybir.AxisListType

P = 128
BANK = 512
EPS = 1e-5

TOP = 10.5

LAG = 3
RING = 4
DVE_SPLITS = (5,)
MAGIC = 0x5F3759DF


def sandwich(nc, x, weight, w_r, w_k, w_v, mu_r, mu_k, out):
    B, T, C = x.shape
    H = weight.shape[0] // C
    HS = C // H
    NB = T // P
    NH = B * H
    UNITS = 8
    SLOTS = NH * UNITS
    BLOCKS = NH * NB
    assert C == P and NB == 8 and HS == 8 and T == 2 * BANK
    ROOT = float(HS) ** 0.5
    VW = 2 * C + 1

    ctx = ExitStack()
    with ctx:
        def sb(name, shape, dt):
            return ctx.enter_context(nc.sbuf_tensor(name, shape, dt))

        def sem(name):
            return ctx.enter_context(nc.semaphore(name))

        ps_s = ctx.enter_context(nc.psum_tensor("ps_s", [P, 2, 2 * BANK], F32))
        ps_o = ctx.enter_context(nc.psum_tensor("ps_o", [P, 2, BANK], F32))
        ps_x = ctx.enter_context(nc.psum_tensor("ps_x", [P, 2 * BANK], F32))

        ident = sb("ident", [P, P], F32)
        ident16 = sb("ident16", [P, P], F16)
        ones = sb("ones", [P, P], F32)
        xin = sb("xin", [P, NB, C], F32)
        w_raw = sb("w_raw", [P, H, C], F32)
        w_hi = sb("w_hi", [P, H * C], F16)
        w_lo = sb("w_lo", [P, H * C], F16)
        wf = sb("wf", [P, 3, C], F32)
        wT = sb("wT", [P, 3, C], F32)
        mu = sb("mu", [P, 2], F32)
        y_hi = sb("y_hi", [P, B * NB, C], F16)
        y_lo = sb("y_lo", [P, B * NB, C], F16)
        yT_hi = sb("yT_hi", [P, B * T], F16)
        yT_lo = sb("yT_lo", [P, B * T], F16)
        shift = sb("shift", [P, NH, NB], F16)
        acc = sb("acc", [P, B * NB, C], F32)
        st_stage = sb("st_stage", [P, 2, 4, 2, 2, 32], F16)
        mv_stage = sb("mv_stage", [P, 2, 4, 2, 2, 32], F16)
        st_op = sb("st_op", [P, 2, 4 * P], F16)
        mv_op = sb("mv_op", [P, 2, 4 * P], F16)
        e_f = sb("e_f", [P, RING, 2 * BANK], F32)
        e_hi = sb("e_hi", [P, 4, NB, BANK], F16)
        e_lo = sb("e_lo", [P, 4, NB, BANK], F16)
        val = sb("val", [P, 2, NB, VW], F16)
        rden = sb("rden", [P, 2, 2], F32)
        tmp = sb("tmp", [P, NB, C], F32)
        x1 = sb("x1", [P, NB, C], F32)
        zT = sb("zT", [P, 1 + T], F32)
        xrT = sb("xrT", [P, T], F32)
        xkT = sb("xkT", [P, T], F32)
        gate = sb("gate", [P, T], F32)
        stats = sb("stats", [P, NB, 6], F32)
        mv = sb("mv", [P, NB, 2], F32)
        nw = sb("nw", [P, 4, NB], F32)
        nwi = sb("nwi", [P, NB], I32)
        n2 = sb("n2", [P, H, NB], F32)
        top2 = sb("top2", [P, H], F32)
        tops = sb("tops", [P, 1], F32)
        diag = sb("diag", [P, H], F32)
        wmm = sb("wmm", [P, 2], F32)
        wmx = sb("wmx", [P, 2], F32)
        ws = sb("ws", [P, 2], F32)

        w_in, f_in = sem("w_in"), sem("f_in")
        x_in = sem("x_in")
        const_ok, pool_zero = sem("const_ok"), sem("pool_zero")
        dve_step = sem("dve_step")
        w_ready = sem("w_ready")
        w_max, w_row, w_top, w_bc = sem("w_max"), sem("w_row"), sem("w_top"), sem("w_bc")
        f_turned, f_ready = sem("f_turned"), sem("f_ready")
        y_split, y_turned, yT_ready = sem("y_split"), sem("y_turned"), sem("yT_ready")
        top_part, top_row, top_diag, top_bc = sem("top_part"), sem("top_row"), sem("top_diag"), sem("top_bc")
        bound2, bound, shift_ready = sem("bound2"), sem("bound"), sem("shift_ready")
        x_used = sem("x_used")
        staged, turned, operands = sem("staged"), sem("turned"), sem("operands")
        scores, weights_f = sem("scores"), sem("weights_f")
        rounded_a, rounded_v, split = sem("rounded_a"), sem("rounded_v"), sem("split")
        values, val_hi, val_lo = sem("values"), sem("val_hi"), sem("val_lo")
        product, den_ok, added = sem("product"), sem("den_ok"), sem("added")
        z_ready, z_turned, zT_ready = sem("z_ready"), sem("z_turned"), sem("zT_ready")
        mixed, gate_ps, key_ps = sem("mixed"), sem("gate_ps"), sem("key_ps")
        gate_e, key_relu, key_ok, kv_ps = sem("gate_e"), sem("key_relu"), sem("key_ok"), sem("kv_ps")
        y_out, stored = sem("y_out"), sem("stored")

        x_v = x.rearrange("b (k p) c -> p b k c", p=P)
        out_v = out.rearrange("b (k p) c -> p b k c", p=P)

        def f16(ap):
            return ap.bitcast(F16)

        def ge(eng, s, value):
            if isinstance(value, int) and value <= 0:
                return
            eng.wait_ge(s, value)

        def live(i, total):
            return not isinstance(i, int) or 0 <= i < total

        def at(it, kl, per):
            return 2 * UNITS // per * it + kl // per

        ACT_SPLITS = tuple(u for u in range(UNITS) if u not in DVE_SPLITS)

        def splits_before(group, n, u):
            return n * len(group) + sum(1 for g in group if g <= u)

        block = ctx.enter_context(nc.Block())

        @block.sync
        def _(sp):
            sp.dma_start(w_raw[:], weight.rearrange("(h c) d -> c h d", c=C)).then_inc(w_in, 16)
            for i, w in enumerate((w_r, w_k, w_v)):
                sp.dma_start(wf[:, i, :], w).then_inc(f_in, 16)
            sp.dma_start(mu[:, 0:1], mu_r.rearrange("(c o) -> c o", o=1)).then_inc(f_in, 16)
            sp.dma_start(mu[:, 1:2], mu_k.rearrange("(c o) -> c o", o=1)).then_inc(f_in, 16)
            sp.dma_start(xin[:], x_v[:, 0]).then_inc(x_in, 16)
            for b in range(1, B):
                sp.wait_ge(x_used, b)
                sp.dma_start(xin[:], x_v[:, b]).then_inc(x_in, 16)
            for b in range(B):
                sp.wait_ge(x_used, B + b)
                sp.dma_start(xin[:], x_v[:, b]).then_inc(x_in, 16)
                sp.wait_ge(y_out, b + 1)
                sp.dma_start(out_v[:, b], tmp[:]).then_inc(stored, 16)
            sp.wait_ge(stored, 16 * B)

        @block.gpsimd
        def _(pool):
            nc.gpsimd.memset(ones[:], 1.0)
            nc.gpsimd.memset(ident[:], 0.0)
            nc.gpsimd.memset(acc[:], 0.0)
            nc.gpsimd.memset(zT[:, 0:1], 0.0)
            nc.gpsimd.memset(val[:], 1.0)
            nc.gpsimd.memset(mv_stage[:], 0.0)
            nc.gpsimd.memset(st_stage[:], 0.0).then_inc(pool_zero, 1)
            pool.wait_ge(pool_zero, 1)
            nc.gpsimd.memset(st_stage[:, :, :, :, :, 3 * HS:3 * HS + 1], 1.0)
            nc.gpsimd.affine_select(out=ident[:], in_=ident[:], compare_op=ALU.not_equal, fill=1.0, base=0,
                                    pattern=[[-1, P]], channel_multiplier=1).then_inc(pool_zero, 1)
            pool.wait_ge(pool_zero, 2)
            nc.gpsimd.tensor_copy(ident16[:], ident[:]).then_inc(const_ok, 1)

            def stage(n, par):
                ge(pool, turned, n - 1)
                pool.nop()

                def parts(a):
                    k0, c0 = n // H * NB + 4 * a, n % H * HS
                    return (y[:, bass.ds(k0, 4), bass.ds(c0, HS)] for y in (y_hi, y_lo))

                last = None
                for a in range(2):
                    hi, lo = parts(a)
                    for d in range(2):
                        for i, part in enumerate((hi, hi, lo)):
                            nc.gpsimd.tensor_copy(st_stage[:, par, :, a, d, HS * i:HS * i + HS], part)
                        for i, part in enumerate((hi, lo, hi)):
                            nc.gpsimd.tensor_copy(mv_stage[:, par, :, d, a, HS * i:HS * i + HS], part)
                        last = nc.gpsimd.tensor_copy(mv_stage[:, par, :, d, a, 3 * HS:3 * HS + 1],
                                                     shift[:, n, 4 * a:4 * a + 4].unsqueeze(2))
                last.then_inc(staged, 1)

            pool.wait_ge(shift_ready, B)
            stage(0, 0)
            stage(1, 1)
            with pool.Fori(1, NH // 2) as it:
                for par in range(2):
                    stage(2 * it + par, par)

        @block.tensor
        def _(pe):
            pe.wait_ge(const_ok, 1)
            pe.wait_ge(w_max, 1)
            nc.tensor.transpose(ps_x[0:1, 0:P], wmx[:, 0:1], ident[:]).then_inc(w_row, 1)
            pe.wait_ge(w_top, 1)
            nc.tensor.matmul(ps_x[:, BANK:BANK + 1], ones[0:1, :], ws[0:1, 0:1], start=True, stop=True).then_inc(w_bc, 1)
            pe.wait_ge(f_in, 80)
            for i in range(3):
                mm = nc.tensor.transpose(ps_o[:, 0, i * P:(i + 1) * P], wf[:, i, :], ident[:])
            mm.then_inc(f_turned, 1)

            def turn_y(b):
                pe.wait_ge(y_split, b + 1)
                ge(pe, yT_ready, 2 * b)
                for k in range(NB):
                    for part, src in enumerate((y_hi, y_lo)):
                        mm = nc.tensor.transpose(f16(ps_s[:, part, 0:BANK])[:, k * P:(k + 1) * P],
                                                 src[:, b * NB + k, :], ident16[:])
                mm.then_inc(y_turned, 1)
                pe.wait_ge(top_part, b + 1)
                nc.tensor.transpose(ps_x[0:H, 0:P], top2[:], ident[:]).then_inc(top_row, 1)
                pe.wait_ge(top_diag, b + 1)
                nc.tensor.matmul(ps_x[:, BANK:BANK + H], ones[0:H, :], diag[0:H, :],
                                 start=True, stop=True).then_inc(top_bc, 1)

            for b in range(B):
                turn_y(b)
            pe.wait_ge(bound2, B)
            pe.wait_ge(yT_ready, 2 * B)
            pe.wait_ge(f_ready, 1)
            pe.wait_ge(w_ready, 1)

            def turn_operands(n, par):
                pe.wait_ge(staged, n + 1)
                ge(pe, val_lo, n)
                for j in range(4):
                    nc.tensor.transpose(f16(ps_x[:, 0:BANK])[:, j * P:(j + 1) * P],
                                        st_stage[:, par, j].rearrange("p a b k -> p (a b k)"), ident16[:])
                for j in range(4):
                    mm = nc.tensor.transpose(f16(ps_x[:, 0:BANK])[:, (4 + j) * P:(5 + j) * P],
                                             mv_stage[:, par, j].rearrange("p a b k -> p (a b k)"), ident16[:])
                mm.then_inc(turned, 1)

            def score_unit(k, u, par):
                half, j = u // 4, u % 4
                ge(pe, weights_f, k - 1)
                for a in range(2):
                    g = 32 * (2 * a + half)
                    mm = nc.tensor.matmul(ps_s[:, u % 2, a * BANK:(a + 1) * BANK],
                                          st_op[g:g + 32, par, j * P:(j + 1) * P],
                                          mv_op[g:g + 32, par, :], start=True, stop=True)
                mm.then_inc(scores, 1)

            def head_values(b, h):
                for pos in range(NB):
                    j, a = pos // 2, pos % 2
                    t0 = b * T + (j + 4 * a) * P
                    dst = ps_x[:, pos * C:(pos + 1) * C]
                    nc.tensor.matmul(dst, yT_hi[:, bass.ds(t0, P)], w_hi[:, bass.ds(h * C, C)], start=True, stop=False)
                    nc.tensor.matmul(dst, yT_hi[:, bass.ds(t0, P)], w_lo[:, bass.ds(h * C, C)], start=False, stop=False)
                    mm = nc.tensor.matmul(dst, yT_lo[:, bass.ds(t0, P)], w_hi[:, bass.ds(h * C, C)], start=False, stop=True)
                mm.then_inc(values, 1)

            def products(it, ql):
                m, i = (ql // 4) % 4, ql % 4
                vp, bank, col = (ql // 8) % 2, (ql // 2) % 2, (ql % 2) * (BANK // 2)
                if i == 0:
                    pe.wait_ge(split, at(it, ql, 1) + 4)
                if ql % 8 == 0:
                    pe.wait_ge(val_lo, at(it, ql, 8) + 1)
                if ql % 2 == 0:
                    ge(pe, added, at(it, ql, 2) - 1)
                for s in range(NB):
                    hi, lo = (e[:, m, s, i * P:(i + 1) * P] for e in (e_hi, e_lo))
                    nc.tensor.matmul(ps_o[:, bank, col:col + C + 1], hi, val[:, vp, s, 0:C + 1],
                                     start=(s == 0), stop=False)
                    nc.tensor.matmul(ps_o[:, bank, col:col + C], hi, val[:, vp, s, C + 1:VW],
                                     start=False, stop=False)
                    mm = nc.tensor.matmul(ps_o[:, bank, col:col + C + 1], lo, val[:, vp, s, 0:C + 1],
                                          start=False, stop=(s == NB - 1))
                if ql % 2 == 1:
                    mm.then_inc(product, 1)

            def pair(it):
                for kk in range(2 * UNITS):
                    k, n, u, par = at(it, kk, 1), at(it, kk, UNITS), kk % UNITS, kk // UNITS
                    if live(k, SLOTS):
                        if u == 0:
                            pe.wait_ge(operands, n + 1)
                        score_unit(k, u, par)
                    if live(at(it, kk - 4 - LAG, 1), BLOCKS):
                        products(it, kk - 4 - LAG)
                    if u == 1 and live(k, SLOTS):
                        head_values(n // H, n % H)
                    if u == 5 and live(k + UNITS, SLOTS):
                        turn_operands(n + 1, 1 - par)

            turn_operands(0, 0)
            pair(0)
            with pe.Fori(1, NH // 2 - 1) as it:
                pair(it)
            pair(NH // 2 - 1)
            pair(NH // 2)

            for b in range(B):
                pe.wait_ge(z_ready, b + 1)
                for k in range(NB):
                    mm = nc.tensor.transpose(ps_s[:, 0, k * P:(k + 1) * P], tmp[:, k, :], ident[:])
                mm.then_inc(z_turned, 1)
                pe.wait_ge(mixed, b + 1)
                for k in range(NB):
                    mm = nc.tensor.matmul(ps_s[:, 1, k * P:(k + 1) * P], xrT[:, k * P:(k + 1) * P], wT[:, 0, :],
                                          start=True, stop=True)
                mm.then_inc(gate_ps, 1)
                for k in range(2):
                    mm = nc.tensor.matmul(ps_s[:, 0, k * BANK:(k + 1) * BANK], wT[:, 1, :],
                                          xkT[:, k * BANK:(k + 1) * BANK], start=True, stop=True)
                mm.then_inc(key_ps, 1)
                pe.wait_ge(key_ok, b + 1)
                for k in range(NB):
                    mm = nc.tensor.matmul(ps_x[:, k * P:(k + 1) * P], xkT[:, k * P:(k + 1) * P], wT[:, 2, :],
                                          start=True, stop=True)
                mm.then_inc(kv_ps, 1)

        @block.scalar
        def _(act):
            for b in range(B):
                act.wait_ge(y_turned, b + 1)
                nc.scalar.activation(yT_hi[:, b * T:(b + 1) * T], f16(ps_s[:, 0, 0:BANK]), ACT.Copy).then_inc(yT_ready, 1)
                nc.scalar.activation(yT_lo[:, b * T:(b + 1) * T], f16(ps_s[:, 1, 0:BANK]), ACT.Copy).then_inc(yT_ready, 1)
                act.wait_ge(bound2, b + 1)
                nc.scalar.activation(n2[:], n2[:], ACT.Sqrt).then_inc(bound, 1)

            def weigh(k, u):
                act.wait_ge(scores, k + 1)
                ge(act, split, k - RING + 1)
                nc.scalar.activation(e_f[:, u % RING, :], ps_s[:, u % 2, :], ACT.Exp,
                                     scale=1.0 / ROOT).then_inc(weights_f, 1)

            def round_hi(it, kl):
                u, m = kl % UNITS, (kl // 4) % 4
                if u not in ACT_SPLITS:
                    return
                act.wait_ge(weights_f, at(it, kl, 1) + 1)
                if kl % 4 == 0 or u - 1 not in ACT_SPLITS:
                    ge(act, product, 2 * at(it, kl, 4) - 6)
                j = kl % 4
                nc.scalar.activation(e_hi[:, m, 2 * j:2 * j + 2, :].rearrange("p s t -> p (s t)"),
                                     e_f[:, kl % RING, :], ACT.Copy).then_inc(rounded_a, 1)

            def pair(it):
                for kk in range(2 * UNITS):
                    k, n, u, par = at(it, kk, 1), at(it, kk, UNITS), kk % UNITS, kk // UNITS
                    if live(k, SLOTS):
                        weigh(k, u)
                    if live(at(it, kk - 1, 1), SLOTS):
                        round_hi(it, kk - 1)
                    if u == 2 and live(k, SLOTS):
                        act.wait_ge(values, n + 1)
                        ge(act, product, 4 * n - 4)
                        nc.scalar.activation(val[:, par, :, 0:C], ps_x[:].rearrange("p (s c) -> p s c", c=C),
                                             ACT.Copy).then_inc(val_hi, 1)

            pair(0)
            with act.Fori(1, NH // 2 - 1) as it:
                pair(it)
            pair(NH // 2 - 1)
            pair(NH // 2)

            for b in range(B):
                act.wait_ge(gate_ps, b + 1)
                nc.scalar.activation(gate[:], ps_s[:, 1, :], ACT.Exp, scale=-1.0).then_inc(gate_e, 1)
                act.wait_ge(key_ps, b + 1)
                nc.scalar.activation(xkT[:], ps_s[:, 0, :], ACT.Relu).then_inc(key_relu, 1)

        @block.vector
        def _(dve):
            steps = [0]

            def step(ins):
                steps[0] += 1
                ins.then_inc(dve_step, 1)
                dve.wait_ge(dve_step, steps[0])

            def inv_root(var):
                ve, y, a, c = (nw[:, i, :] for i in range(4))
                step(dve.tensor_scalar(ve, var, EPS, None, ALU.add))
                step(dve.tensor_scalar(nwi[:], ve.bitcast(I32), 1, None, ALU.logical_shift_right))
                step(dve.tensor_scalar(y.bitcast(I32), nwi[:], -1.0, float(MAGIC), ALU.mult, ALU.add))
                for _ in range(3):
                    step(dve.scalar_tensor_tensor(out=a, in0=y, scalar=-0.5, in1=y, op0=ALU.mult, op1=ALU.mult))
                    step(dve.tensor_tensor(c, a, ve, ALU.mult))
                    step(dve.scalar_tensor_tensor(out=y, in0=c, scalar=1.5, in1=y, op0=ALU.add, op1=ALU.mult))

            def layer_norm(dst, src):
                for k in range(NB):
                    i = dve.bn_stats(stats[:, k, :], src[:, k, :])
                step(i)
                for k in range(NB):
                    i = dve.bn_aggr(mv[:, k, :], stats[:, k, :])
                step(i)
                inv_root(mv[:, :, 1])
                for k in range(NB):
                    i = dve.tensor_scalar(dst[:, k, :], src[:, k, :], mv[:, k, 0:1], nw[:, 1, k:k + 1],
                                          ALU.subtract, ALU.mult)
                return i

            dve.wait_ge(w_in, 16)
            dve.tensor_reduce(wmm[:, 0:1], w_raw[:], AX.XY, ALU.max)
            step(dve.tensor_reduce(wmm[:, 1:2], w_raw[:], AX.XY, ALU.min))
            dve.scalar_tensor_tensor(out=wmx[:, 0:1], in0=wmm[:, 1:2], scalar=-1.0, in1=wmm[:, 0:1],
                                     op0=ALU.mult, op1=ALU.max).then_inc(w_max, 1)
            dve.wait_ge(w_row, 1)
            step(dve.tensor_reduce(wmm[0:1, 0:1], ps_x[0:1, 0:P], AX.X, ALU.max))
            step(dve.tensor_scalar(wmm[0:1, 1:2], wmm[0:1, 0:1], 1e-30, None, ALU.max))
            dve.tensor_scalar(ws[0:1, 0:1].bitcast(I32), wmm[0:1, 1:2].bitcast(I32), 0x7F800000, None,
                              ALU.bitwise_and).then_inc(w_top, 1)
            dve.wait_ge(w_bc, 1)
            step(dve.tensor_copy(ws[:, 0:1], ps_x[:, BANK:BANK + 1]))
            step(dve.reciprocal(ws[:, 1:2], ws[:, 0:1]))
            w_flat = w_raw[:].rearrange("p h c -> p (h c)")
            step(dve.tensor_scalar(w_flat, w_flat, ws[:, 1:2], None, ALU.mult))
            step(dve.tensor_copy(w_hi[:], w_flat))
            dve.tensor_tensor(w_lo[:], w_flat, w_hi[:], ALU.subtract).then_inc(w_ready, 1)
            dve.wait_ge(f_turned, 1)
            dve.tensor_copy(wT[:].rearrange("p i c -> p (i c)"), ps_o[:, 0, 0:3 * P]).then_inc(f_ready, 1)

            for b in range(B):
                heads = slice(b * H, (b + 1) * H)
                dve.wait_ge(x_in, 16 * (b + 1))
                step(layer_norm(tmp, xin))
                hi, lo = y_hi[:, b * NB:(b + 1) * NB, :], y_lo[:, b * NB:(b + 1) * NB, :]
                dve.tensor_copy(hi, tmp[:]).then_inc(x_used, 1)
                dve.wait_ge(x_used, b + 1)
                dve.tensor_tensor(lo, tmp[:], hi, ALU.subtract).then_inc(y_split, 1)
                step(dve.tensor_tensor(x1[:], tmp[:], tmp[:], ALU.mult))
                step(dve.tensor_reduce(n2[:].rearrange("p h k -> p k h"),
                                       x1[:].rearrange("p k (h c) -> p k h c", c=HS), AX.X, ALU.add))
                dve.tensor_reduce(top2[:], n2[:], AX.X, ALU.max).then_inc(top_part, 1)
                dve.wait_ge(top_row, b + 1)
                step(dve.tensor_reduce(tops[0:H, :], ps_x[0:H, 0:P], AX.X, ALU.max))
                dve.tensor_scalar(diag[0:H, :], ident[0:H, 0:H], tops[0:H, 0:1], None, ALU.mult).then_inc(top_diag, 1)
                dve.wait_ge(top_bc, b + 1)
                step(dve.tensor_copy(top2[:], ps_x[:, BANK:BANK + H]))
                dve.tensor_tensor(n2[:], n2[:], top2[:].unsqueeze(2).to_broadcast([P, H, NB]),
                                  ALU.mult).then_inc(bound2, 1)
                dve.wait_ge(bound, b + 1)
                dve.tensor_scalar(shift[:, heads], n2[:], -1.0, TOP * ROOT, ALU.mult, ALU.add).then_inc(shift_ready, 1)
                dve.wait_ge(shift_ready, b + 1)

            def split_unit(it, kl):
                n, u, m, j = at(it, kl, UNITS), kl % UNITS, (kl // 4) % 4, kl % 4
                hi, lo = (e[:, m, 2 * j:2 * j + 2, :].rearrange("p s t -> p (s t)") for e in (e_hi, e_lo))
                ge(dve, product, 2 * at(it, kl, 4) - 6)
                if u in DVE_SPLITS:
                    dve.wait_ge(weights_f, at(it, kl, 1) + 1)
                    dve.tensor_copy(hi, e_f[:, kl % RING, :]).then_inc(rounded_v, 1)
                    dve.wait_ge(rounded_v, splits_before(DVE_SPLITS, n, u))
                else:
                    dve.wait_ge(rounded_a, splits_before(ACT_SPLITS, n, u))
                dve.tensor_tensor(lo, e_f[:, kl % RING, :], hi, ALU.subtract).then_inc(split, 1)

            def add_pair(it, ql):
                bank, r = (ql // 2) % 2, at(it, ql, 2)
                b = at(it, ql, UNITS) // H
                dve.wait_ge(product, r + 1)
                dve.reciprocal(rden[:, bank, :], ps_o[:, bank, C:C + BANK // 2 + 1:BANK // 2]).then_inc(den_ok, 1)
                dve.wait_ge(den_ok, r + 1)
                ge(dve, added, r)
                for i in range(2):
                    dst = acc[:, bass.ds(b * NB + (ql - 1 + i) % 8, 1), :].rearrange("p a c -> p (a c)")
                    ins = dve.scalar_tensor_tensor(out=dst, in0=ps_o[:, bank, i * BANK // 2:i * BANK // 2 + C],
                                                   scalar=rden[:, bank, i:i + 1], in1=dst,
                                                   op0=ALU.mult, op1=ALU.add)
                ins.then_inc(added, 1)

            def pair(it):
                for kk in range(2 * UNITS):
                    k, n, u, par = at(it, kk, 1), at(it, kk, UNITS), kk % UNITS, kk // UNITS
                    if live(at(it, kk - 2, 1), SLOTS):
                        split_unit(it, kk - 2)
                    if (kk - 5 - LAG) % 2 == 1 and live(at(it, kk - 5 - LAG, 1), BLOCKS):
                        add_pair(it, kk - 5 - LAG)
                    if u == 3 and live(k, SLOTS):
                        dve.wait_ge(val_hi, n + 1)
                        dve.tensor_tensor(val[:, par, :, C + 1:VW], ps_x[:].rearrange("p (s c) -> p s c", c=C),
                                          val[:, par, :, 0:C], ALU.subtract).then_inc(val_lo, 1)
                    if u == 6 and live(k + UNITS, SLOTS):
                        take_operands(n + 1, 1 - par)

            def take_operands(n, par):
                dve.wait_ge(turned, n + 1)
                ge(dve, scores, UNITS * (n - 1))
                dve.tensor_copy(st_op[:, par, :], f16(ps_x[:, 0:BANK])[:, 0:4 * P])
                dve.tensor_copy(mv_op[:, par, :], f16(ps_x[:, 0:BANK])[:, 4 * P:8 * P]).then_inc(operands, 1)

            dve.wait_ge(const_ok, 1)
            take_operands(0, 0)
            pair(0)
            with dve.Fori(1, NH // 2 - 1) as it:
                pair(it)
            pair(NH // 2 - 1)
            pair(NH // 2)

            dve.wait_ge(added, BLOCKS // 2)
            for b in range(B):
                row = acc[:, b * NB:(b + 1) * NB, :]
                flat = acc[:, b * NB:(b + 1) * NB, :].rearrange("p k c -> p (k c)")
                step(dve.tensor_scalar(flat, flat, ws[:, 0:1], None, ALU.mult))
                step(layer_norm(row, row))
                dve.wait_ge(x_in, 16 * (B + b + 1))
                dve.tensor_tensor(x1[:], row, xin[:], ALU.add).then_inc(x_used, 1)
                dve.wait_ge(x_used, B + b + 1)
                ge(dve, stored, 16 * b)
                layer_norm(tmp, x1).then_inc(z_ready, 1)
                dve.wait_ge(z_turned, b + 1)
                step(dve.tensor_copy(zT[:, 1:1 + T], ps_s[:, 0, :]))
                step(dve.tensor_tensor(xrT[:], zT[:, 1:1 + T], zT[:, 0:T], ALU.subtract))
                dve.scalar_tensor_tensor(out=xkT[:], in0=xrT[:], scalar=mu[:, 1:2], in1=zT[:, 0:T],
                                         op0=ALU.mult, op1=ALU.add)
                dve.scalar_tensor_tensor(out=xrT[:], in0=xrT[:], scalar=mu[:, 0:1], in1=zT[:, 0:T],
                                         op0=ALU.mult, op1=ALU.add).then_inc(mixed, 1)
                dve.wait_ge(gate_e, b + 1)
                step(dve.tensor_scalar(gate[:], gate[:], 1.0, None, ALU.add))
                step(dve.reciprocal(gate[:], gate[:]))
                dve.wait_ge(key_relu, b + 1)
                dve.tensor_tensor(xkT[:], xkT[:], xkT[:], ALU.mult).then_inc(key_ok, 1)
                dve.wait_ge(kv_ps, b + 1)
                g3 = gate[:].rearrange("p (k c) -> p k c", c=C)
                step(dve.tensor_tensor(gate[:], gate[:], ps_x[:], ALU.mult))
                step(layer_norm(tmp, g3))
                dve.tensor_tensor(tmp[:], tmp[:], x1[:], ALU.add).then_inc(y_out, 1)
                dve.wait_ge(y_out, b + 1)


_INS = ['L0_attn_x', 'L0_attn_weight', 'L0_ffn_W_r', 'L0_ffn_W_k', 'L0_ffn_W_v', 'L0_ffn_mu_r', 'L0_ffn_mu_k']


def kernel(**inputs):
    import numpy as _np
    import concourse.bacc as _bacc
    from concourse import mybir as _mybir
    from concourse.bass_utils import run_bass_kernel_spmd as _run

    nc = _bacc.Bacc("TRN2", target_bir_lowering=False, num_devices=1)
    arrays, args = {}, []
    for name in _INS:
        a = _np.ascontiguousarray(inputs[name])
        arrays[f"in_{name}_dram"] = a
        args.append(nc.dram_tensor(f"in_{name}_dram", a.shape, _mybir.dt.from_np(a.dtype), kind="ExternalInput").ap())
    shape = _np.shape(inputs['L0_attn_x'])
    args.append(nc.dram_tensor("out_0_dram", shape, _mybir.dt.float32, kind="ExternalOutput").ap())
    sandwich(nc, *args)
    r = _run(nc, [arrays], core_ids=[0])
    return r.results[0]["out_0_dram"]
```

```python
from contextlib import ExitStack

import concourse.bass as bass
from concourse import mybir

F32 = mybir.dt.float32
F16 = mybir.dt.float16
I32 = mybir.dt.int32
ALU = mybir.AluOpType
ACT = mybir.ActivationFunctionType
AX = mybir.AxisListType

P = 128
BANK = 512
EPS = 1e-5

TOP = 10.5

LAG = 7
RING = 4
DVE_SPLITS = (5,)
MAGIC = 0x5F3759DF


def sandwich(nc, x, weight, w_r, w_k, w_v, mu_r, mu_k, out):
    B, T, C = x.shape
    H = weight.shape[0] // C
    HS = C // H
    NB = T // P
    NH = B * H
    UNITS = 8
    SLOTS = NH * UNITS
    BLOCKS = NH * NB
    assert C == P and NB == 8 and HS == 8 and T == 2 * BANK
    ROOT = float(HS) ** 0.5
    VW = 2 * C + 1

    ctx = ExitStack()
    with ctx:
        def sb(name, shape, dt):
            return ctx.enter_context(nc.sbuf_tensor(name, shape, dt))

        def sem(name):
            return ctx.enter_context(nc.semaphore(name))

        ps_s = ctx.enter_context(nc.psum_tensor("ps_s", [P, 2, 2 * BANK], F32))
        ps_o = ctx.enter_context(nc.psum_tensor("ps_o", [P, 2, BANK], F32))
        ps_x = ctx.enter_context(nc.psum_tensor("ps_x", [P, 2 * BANK], F32))

        ident = sb("ident", [P, P], F32)
        ident16 = sb("ident16", [P, P], F16)
        ones = sb("ones", [P, P], F32)
        xs = sb("xs", [P, B * NB, C], F32)
        w_raw = sb("w_raw", [P, H, C], F32)
        w_hi = sb("w_hi", [P, H * C], F16)
        w_lo = sb("w_lo", [P, H * C], F16)
        wf = sb("wf", [P, 3, C], F32)
        wT = sb("wT", [P, 3, C], F32)
        mu = sb("mu", [P, 2], F32)
        y_hi = sb("y_hi", [P, B * NB, C], F16)
        y_lo = sb("y_lo", [P, B * NB, C], F16)
        yT_hi = sb("yT_hi", [P, B * T], F16)
        yT_lo = sb("yT_lo", [P, B * T], F16)
        shift = sb("shift", [P, NH, NB], F16)
        acc = sb("acc", [P, B * NB, C], F32)
        st_stage = sb("st_stage", [P, 2, 4, 2, 2, 32], F16)
        mv_stage = sb("mv_stage", [P, 2, 4, 2, 2, 32], F16)
        op = sb("op", [P, 2, 8 * P], F16)
        e_f = sb("e_f", [P, RING, 2 * BANK], F32)
        e_hi = sb("e_hi", [P, 4, NB, BANK], F16)
        e_lo = sb("e_lo", [P, 4, NB, BANK], F16)
        val = sb("val", [P, 2, NB, VW], F16)
        rden = sb("rden", [P, 2, 2], F32)
        tmp = sb("tmp", [P, NB, C], F32)
        zT = sb("zT", [P, 1 + T], F32)
        xrT, xkT = (w_raw[:].rearrange("p h c -> p (h c)")[:, i * T:(i + 1) * T] for i in range(2))
        gate = sb("gate", [P, T], F32)
        sq = gate[:].rearrange("p (k c) -> p k c", c=C)
        keep = sb("keep", [P, B * NB], F32)
        zb = sb("zb", [P, C], F32)
        zTb = sb("zTb", [P, 1 + P], F32)
        mixb = sb("mixb", [P, 3, P], F32)
        actb = sb("actb", [P, 2, P], F32)
        gb = sb("gb", [P, C], F32)
        ob = sb("ob", [P, C], F32)
        bst = sb("bst", [P, 3, 6], F32)
        bmv = sb("bmv", [P, 3, 2], F32)
        bnw = sb("bnw", [P, 3, 4], F32)
        ab = sb("ab", [P, 2, C], F32)
        consts = sb("consts", [P, 3], F32)
        idle = sb("idle", [P, 6], F32)
        stats = sb("stats", [P, NB, 6], F32)
        mv = sb("mv", [P, NB, 2], F32)
        nw = sb("nw", [P, 4, NB], F32)
        nwi = sb("nwi", [P, NB], I32)
        n2 = sb("n2", [P, H, NB], F32)
        top2 = sb("top2", [P, H], F32)
        tops = sb("tops", [P, 1], F32)
        diag = sb("diag", [P, H], F32)
        wmm = sb("wmm", [P, 2], F32)
        wmx = sb("wmx", [P, 2], F32)
        ws = sb("ws", [P, 2], F32)

        w_in, f_in = sem("w_in"), sem("f_in")
        x_in = [sem(f"x_in_{b}") for b in range(B)]
        const_ok, pool_zero = sem("const_ok"), sem("pool_zero")
        dve_step = sem("dve_step")
        w_scale, w_rounded, w_ready = sem("w_scale"), sem("w_rounded"), sem("w_ready")
        w_max, w_row, w_top, w_bc = sem("w_max"), sem("w_row"), sem("w_top"), sem("w_bc")
        f_turned, f_ready = sem("f_turned"), sem("f_ready")
        y_split, y_turned, yT_ready = sem("y_split"), sem("y_turned"), sem("yT_ready")
        top_part, top_row, top_diag, top_bc = sem("top_part"), sem("top_row"), sem("top_diag"), sem("top_bc")
        bound2, shift_ready, zero_ok = sem("bound2"), sem("shift_ready"), sem("zero_ok")
        squared, row_summed = sem("squared"), sem("row_summed")
        staged, turned, operands = sem("staged"), sem("turned"), sem("operands")
        scores, weights_f = sem("scores"), sem("weights_f")
        rounded_a, rounded_v, split = sem("rounded_a"), sem("rounded_v"), sem("split")
        values, val_hi, val_lo = sem("values"), sem("val_hi"), sem("val_lo")
        product, den_ok, added = sem("product"), sem("den_ok"), sem("added")
        z_ready, z_turned, zT_ready = sem("z_ready"), sem("z_turned"), sem("zT_ready")
        mixed, gate_ps, key_ps = sem("mixed"), sem("gate_ps"), sem("key_ps")
        gate_e, key_relu, key_ok, kv_ps = sem("gate_e"), sem("key_relu"), sem("key_ok"), sem("kv_ps")
        y_out, stored = sem("y_out"), sem("stored")
        root = [sem(f"root_{i}") for i in range(3)]
        ROOT_STEPS = 7
        b_sum = [sem(f"b_sum_{i}") for i in range(3)]
        b_mean = [sem(f"b_mean_{i}") for i in range(3)]
        b_scaled = sem("b_scaled")
        b_norm, b_x1, b_z, b_turned, b_prev = (sem(x) for x in ("b_norm", "b_x1", "b_z", "b_turned", "b_prev"))
        b_zT, b_diff, b_mixed, b_proj, b_act = (sem(x) for x in ("b_zT", "b_diff", "b_mixed", "b_proj", "b_act"))
        b_act1, b_gate, b_kv, b_gated = (sem(x) for x in ("b_act1", "b_gate", "b_kv", "b_gated"))
        b_res, b_out, b_stored = (sem(x) for x in ("b_res", "b_out", "b_stored"))

        x_v = x.rearrange("b (k p) c -> p b k c", p=P)
        out_v = out.rearrange("b (k p) c -> p b k c", p=P)
        out_b = out.rearrange("b (k p) c -> (b k) p c", p=P)
        EARLY = (B - 1) * NB
        PAIRS = NH // 2
        ROW = H // 2
        assert ROW == NB

        def f16(ap):
            return ap.bitcast(F16)

        def ge(eng, s, value):
            if isinstance(value, int) and value <= 0:
                return
            eng.wait_ge(s, value)

        def live(i, total):
            return not isinstance(i, int) or 0 <= i < total

        def at(it, kl, per):
            return 2 * UNITS // per * it + kl // per

        def heads_done(n):
            return min(n + 1, NH) if isinstance(n, int) else n + 1

        def at_block(it):
            return it - ROW

        def run(eng, pair):
            for it in range(B - 1):
                pair(it, False)
            with eng.Fori(B - 1, ROW) as it:
                pair(it, False)
            pair(ROW, True)
            with eng.Fori(ROW + 1, PAIRS - 1) as it:
                pair(it, True)
            pair(PAIRS - 1, True)
            pair(PAIRS, True)

        ACT_SPLITS = tuple(u for u in range(2 * UNITS) if u not in DVE_SPLITS)

        def rounded(group, it, kl):
            u = kl % (2 * UNITS)
            return at(it, kl, 2 * UNITS) * len(group) + sum(1 for g in group if g <= u)

        block = ctx.enter_context(nc.Block())

        @block.sync
        def _(sp):
            sp.dma_start(xs[:, 0:NB, :], x_v[:, 0]).then_inc(x_in[0], 16)
            sp.dma_start(w_raw[:], weight.rearrange("(h c) d -> c h d", c=C)).then_inc(w_in, 16)
            for i, w in enumerate((w_r, w_k, w_v)):
                sp.dma_start(wf[:, i, :], w).then_inc(f_in, 16)
            sp.dma_start(mu[:, 0:1], mu_r.rearrange("(c o) -> c o", o=1)).then_inc(f_in, 16)
            sp.dma_start(mu[:, 1:2], mu_k.rearrange("(c o) -> c o", o=1)).then_inc(f_in, 16)
            for b in range(1, B):
                sp.dma_start(xs[:, b * NB:(b + 1) * NB, :], x_v[:, b]).then_inc(x_in[b], 16)
            with sp.Fori(0, EARLY) as q:
                sp.wait_ge(b_out, q + 1)
                sp.dma_start(out_b[bass.ds(q, 1)].rearrange("q p c -> p (q c)"), ob[:]).then_inc(b_stored, 16)
            sp.wait_ge(y_out, 1)
            sp.dma_start(out_v[:, B - 1], tmp[:]).then_inc(stored, 16)
            sp.wait_ge(stored, 16)
            sp.wait_ge(b_stored, 16 * EARLY)

        @block.gpsimd
        def _(pool):
            nc.gpsimd.memset(ident[:], 0.0)
            nc.gpsimd.memset(mv_stage[:], 0.0)
            nc.gpsimd.memset(st_stage[:], 0.0)
            nc.gpsimd.memset(val[:, :, :, C:C + 1], 1.0)
            nc.gpsimd.memset(keep[:], 1.0)
            nc.gpsimd.memset(consts[:, 0:1], EPS)
            nc.gpsimd.memset(consts[:, 1:2], 1.5)
            nc.gpsimd.memset(consts[:, 2:3], -0.5)
            nc.gpsimd.memset(zTb[:], 0.0)
            nc.gpsimd.memset(zT[:, 0:1], 0.0)
            nc.gpsimd.memset(ones[:], 1.0).then_inc(pool_zero, 1)
            pool.wait_ge(pool_zero, 1)
            nc.gpsimd.memset(keep[:, 0:B * NB:NB], 0.0)
            nc.gpsimd.memset(st_stage[:, :, :, :, :, 3 * HS:3 * HS + 1], 1.0)
            nc.gpsimd.affine_select(out=ident[:], in_=ident[:], compare_op=ALU.not_equal, fill=1.0, base=0,
                                    pattern=[[-1, P]], channel_multiplier=1).then_inc(pool_zero, 1)
            pool.wait_ge(pool_zero, 2)
            nc.gpsimd.tensor_copy(ident16[:], ident[:]).then_inc(const_ok, 1)

            def stage(n, par):
                ge(pool, turned, n - 1)
                for a in range(2):
                    k0, c0 = n // H * NB + 4 * a, n % H * HS
                    hi, lo = (y[:, bass.ds(k0, 4), bass.ds(c0, HS)] for y in (y_hi, y_lo))
                    for d in range(2):
                        for i, part in enumerate((hi, hi, lo)):
                            nc.gpsimd.tensor_copy(st_stage[:, par, :, a, d, HS * i:HS * i + HS], part)
                        for i, part in enumerate((hi, lo, hi)):
                            nc.gpsimd.tensor_copy(mv_stage[:, par, :, d, a, HS * i:HS * i + HS], part)
                if isinstance(n, int) and n == 0:
                    pool.wait_ge(shift_ready, 1)
                for a in range(2):
                    for d in range(2):
                        last = nc.gpsimd.tensor_copy(mv_stage[:, par, :, d, a, 3 * HS:3 * HS + 1],
                                                     shift[:, n, 4 * a:4 * a + 4].unsqueeze(2))
                last.then_inc(staged, 1)

            def row_rest(b):
                pool.wait_ge(y_split, 2 * b + 1)
                nc.gpsimd.tensor_tensor(y_lo[:, b * NB:(b + 1) * NB, :], tmp[:], y_hi[:, b * NB:(b + 1) * NB, :],
                                        ALU.subtract).then_inc(y_split, 1)
                pool.wait_ge(shift_ready, b)
                nc.gpsimd.tensor_tensor(sq, tmp[:], tmp[:], ALU.mult).then_inc(squared, 1)

            def deviation(i, q):
                v, y, a = (bnw[:, i, c:c + 1] for c in range(3))
                done = [0]

                def step(out, in0, in1, op):
                    done[0] += 1
                    nc.gpsimd.tensor_tensor(out, in0, in1, op).then_inc(root[i], 1)
                    pool.wait_ge(root[i], q * ROOT_STEPS + done[0])

                pool.wait_ge(b_mean[i], q + 1)
                step(v, bmv[:, i, 1:2], consts[:, 0:1], ALU.add)
                step(y, v, consts[:, 2:3], ALU.pow)
                step(a, y, y, ALU.mult)
                step(a, a, v, ALU.mult)
                step(a, a, consts[:, 2:3], ALU.mult)
                step(a, a, consts[:, 1:2], ALU.add)
                step(y, y, a, ALU.mult)
                assert done[0] == ROOT_STEPS

            def pair(it, ffn):
                q, p = at_block(it), at_block(it) - 1
                if ffn and live(p, EARLY):
                    ge(pool, b_mixed, p)
                    nc.gpsimd.tensor_tensor(zTb[:, 0:1], zTb[:, P:P + 1], keep[:, bass.ds(p, 1)],
                                            ALU.mult).then_inc(b_prev, 1)
                if live(2 * it + 2, NH):
                    stage(2 * it + 2, 0)
                if live(2 * it + 3, NH):
                    stage(2 * it + 3, 1)
                if ffn and live(p, EARLY):
                    pool.wait_ge(b_act, p + 1)
                    nc.gpsimd.tensor_tensor(actb[:, 0, :], actb[:, 0, :], ones[:], ALU.add)
                    nc.gpsimd.tensor_tensor(actb[:, 1, :], actb[:, 1, :], actb[:, 1, :], ALU.mult).then_inc(b_act1, 1)
                if ffn and live(q, EARLY):
                    deviation(0, q)
                    pool.wait_ge(b_norm, q + 1)
                    rows, x_rows = (w[:, bass.ds(q, 1), :].rearrange("p a c -> p (a c)") for w in (acc, xs))
                    nc.gpsimd.tensor_tensor(rows, ab[:, 0, :], x_rows, ALU.add)
                    nc.gpsimd.tensor_tensor(ab[:, 1, :], ab[:, 0, :], x_rows, ALU.add).then_inc(b_x1, 1)
                    deviation(1, q)
                if ffn and live(p, EARLY):
                    deviation(2, p)
                    ge(pool, b_stored, 16 * p)
                    nc.gpsimd.tensor_tensor(ob[:], gb[:], bmv[:, 2, 0:1].to_broadcast([P, C]),
                                            ALU.subtract).then_inc(b_res, 1)
                    pool.wait_ge(b_res, 2 * p + 1)
                    nc.gpsimd.tensor_tensor(ob[:], ob[:], bnw[:, 2, 1:2].to_broadcast([P, C]),
                                            ALU.mult).then_inc(b_res, 1)
                    pool.wait_ge(b_res, 2 * p + 2)
                    nc.gpsimd.tensor_tensor(ob[:], ob[:], acc[:, bass.ds(p, 1), :].rearrange("p a c -> p (a c)"),
                                            ALU.add).then_inc(b_out, 1)
                if isinstance(it, int) and it + 1 < B:
                    row_rest(it + 1)
                    pool.wait_ge(shift_ready, it + 2)

            pool.wait_ge(y_split, 2)
            stage(0, 0)
            stage(1, 1)
            run(pool, pair)

        @block.tensor
        def _(pe):
            pe.wait_ge(const_ok, 1)
            aux = ps_x[:, BANK:2 * BANK]

            def weight_top():
                pe.wait_ge(w_max, 1)
                pe.wait_ge(bound2, 1)
                nc.tensor.transpose(aux[0:1, 0:P], wmx[:, 0:1], ident[:]).then_inc(w_row, 1)
                pe.wait_ge(w_top, 1)
                nc.tensor.matmul(aux[:, P:P + 1], ones[0:1, :], ws[0:1, 0:1], start=True, stop=True).then_inc(w_bc, 1)
                pe.wait_ge(f_in, 80)
                for i in range(3):
                    mm = nc.tensor.transpose(ps_o[:, 0, i * P:(i + 1) * P], wf[:, i, :], ident[:])
                mm.then_inc(f_turned, 1)

            def turn_y(b, part):
                pe.wait_ge(y_split, 2 * b + part + 1)
                ge(pe, bound2, b)
                for k in range(NB):
                    mm = nc.tensor.transpose(f16(aux)[:, k * P:(k + 1) * P],
                                             (y_hi, y_lo)[part][:, b * NB + k, :], ident16[:])
                mm.then_inc(y_turned, 1)

            def turn_top(b):
                pe.wait_ge(top_part, b + 1)
                pe.wait_ge(yT_ready, 2 * b + 1)
                nc.tensor.transpose(aux[0:H, 0:P], top2[:], ident[:]).then_inc(top_row, 1)

            def spread_top(b):
                pe.wait_ge(top_diag, b + 1)
                pe.wait_ge(yT_ready, 2 * b + 2)
                nc.tensor.matmul(aux[:, 0:H], ones[0:H, :], diag[0:H, :], start=True, stop=True).then_inc(top_bc, 1)

            turn_y(0, 0)
            turn_top(0)
            pe.wait_ge(top_diag, 1)
            turn_y(0, 1)
            spread_top(0)

            def turn_operands(n, par):
                pe.wait_ge(staged, n + 1)
                ge(pe, val_lo, 2 * n - 2)
                for j in range(4):
                    nc.tensor.transpose(f16(ps_x[:, 0:BANK])[:, j * P:(j + 1) * P],
                                        st_stage[:, par, j].rearrange("p a b k -> p (a b k)"), ident16[:])
                for j in range(4):
                    mm = nc.tensor.transpose(f16(ps_x[:, 0:BANK])[:, (4 + j) * P:(5 + j) * P],
                                             mv_stage[:, par, j].rearrange("p a b k -> p (a b k)"), ident16[:])
                mm.then_inc(turned, 1)

            def score_unit(k, u, par):
                half, j = u // 4, u % 4
                ge(pe, weights_f, k - 1)
                for a in range(2):
                    g = 32 * (2 * a + half)
                    mm = nc.tensor.matmul(ps_s[:, u % 2, a * BANK:(a + 1) * BANK],
                                          op[g:g + 32, par, j * P:(j + 1) * P],
                                          op[g:g + 32, par, 4 * P:8 * P], start=True, stop=True)
                mm.then_inc(scores, 1)

            def head_values(n, part):
                b, h = n // H, n % H
                if part == 0:
                    ge(pe, operands, heads_done(n + 1))
                else:
                    pe.wait_ge(val_lo, 2 * n + 1)
                for i in range(NB // 2):
                    pos = part * NB // 2 + i
                    j, a = pos // 2, pos % 2
                    t0 = b * T + (j + 4 * a) * P
                    dst = ps_x[:, i * C:(i + 1) * C]
                    nc.tensor.matmul(dst, yT_hi[:, bass.ds(t0, P)], w_hi[:, bass.ds(h * C, C)], start=True, stop=False)
                    nc.tensor.matmul(dst, yT_hi[:, bass.ds(t0, P)], w_lo[:, bass.ds(h * C, C)], start=False, stop=False)
                    mm = nc.tensor.matmul(dst, yT_lo[:, bass.ds(t0, P)], w_hi[:, bass.ds(h * C, C)], start=False, stop=True)
                mm.then_inc(values, 1)

            def products(it, ql):
                m, i = (ql // 4) % 4, ql % 4
                vp, bank, col = (ql // 8) % 2, (ql // 2) % 2, (ql % 2) * (BANK // 2)
                if i == 0:
                    pe.wait_ge(split, at(it, ql, 1) + 4)
                if ql % 8 == 0:
                    pe.wait_ge(val_lo, 2 * at(it, ql, 8) + 2)
                if ql % 2 == 0:
                    ge(pe, added, at(it, ql, 2) - 1)
                for s in range(NB):
                    hi, lo = (e[:, m, s, i * P:(i + 1) * P] for e in (e_hi, e_lo))
                    nc.tensor.matmul(ps_o[:, bank, col:col + C + 1], hi, val[:, vp, s, 0:C + 1],
                                     start=(s == 0), stop=False)
                    nc.tensor.matmul(ps_o[:, bank, col:col + C], hi, val[:, vp, s, C + 1:VW],
                                     start=False, stop=False)
                    mm = nc.tensor.matmul(ps_o[:, bank, col:col + C + 1], lo, val[:, vp, s, 0:C + 1],
                                          start=False, stop=(s == NB - 1))
                if ql % 2 == 1:
                    mm.then_inc(product, 1)

            def pair(it, ffn):
                q, p = at_block(it), at_block(it) - 1
                for kk in range(2 * UNITS):
                    k, n, u, par = at(it, kk, 1), at(it, kk, UNITS), kk % UNITS, kk // UNITS
                    if live(k, SLOTS):
                        if u == 0:
                            pe.wait_ge(operands, n + 1)
                        score_unit(k, u, par)
                    if live(at(it, kk - 4 - LAG, 1), BLOCKS):
                        products(it, kk - 4 - LAG)
                    if u == 1 and live(k + UNITS, SLOTS):
                        turn_operands(n + 1, 1 - par)
                    if u in (3, 6) and live(k, SLOTS):
                        if isinstance(it, int) and k == 3:
                            pe.wait_ge(w_ready, 1)
                        head_values(n, u // 6)
                    if isinstance(it, int) and it + 1 < B:
                        if kk == 7:
                            turn_y(it + 1, 0)
                        if kk == 10:
                            turn_top(it + 1)
                        if kk == 12:
                            pe.wait_ge(top_diag, it + 2)
                            turn_y(it + 1, 1)
                        if kk == 14:
                            spread_top(it + 1)
                    if ffn and live(p, EARLY):
                        if kk == 4:
                            pe.wait_ge(b_z, p + 1)
                            ge(pe, b_gated, p)
                            nc.tensor.transpose(aux[:, 0:P], zb[:], ident[:]).then_inc(b_turned, 1)
                        if kk == 7:
                            pe.wait_ge(b_mixed, p + 1)
                            nc.tensor.matmul(aux[:, P:2 * P], mixb[:, 0, :], wT[:, 0, :], start=True, stop=True)
                            nc.tensor.matmul(aux[:, 2 * P:3 * P], wT[:, 1, :], mixb[:, 1, :],
                                             start=True, stop=True).then_inc(b_proj, 1)
                        if kk == 12:
                            pe.wait_ge(b_act1, p + 1)
                            nc.tensor.matmul(aux[:, 3 * P:4 * P], actb[:, 1, :], wT[:, 2, :],
                                             start=True, stop=True).then_inc(b_kv, 1)

            turn_operands(0, 0)
            weight_top()
            run(pe, pair)

            pe.wait_ge(b_gated, EARLY)
            pe.wait_ge(z_ready, 1)
            for k in range(NB):
                mm = nc.tensor.transpose(ps_s[:, 0, k * P:(k + 1) * P], tmp[:, k, :], ident[:])
            mm.then_inc(z_turned, 1)
            pe.wait_ge(mixed, 1)
            for k in range(2):
                mm = nc.tensor.matmul(ps_s[:, 0, k * BANK:(k + 1) * BANK], wT[:, 1, :],
                                      xkT[:, k * BANK:(k + 1) * BANK], start=True, stop=True)
            mm.then_inc(key_ps, 1)
            pe.wait_ge(mixed, 2)
            for k in range(NB):
                mm = nc.tensor.matmul(ps_s[:, 1, k * P:(k + 1) * P], xrT[:, k * P:(k + 1) * P], wT[:, 0, :],
                                      start=True, stop=True)
            mm.then_inc(gate_ps, 1)
            pe.wait_ge(key_ok, 1)
            pe.wait_ge(val_lo, 2 * NH)
            for k in range(NB):
                mm = nc.tensor.matmul(ps_x[:, k * P:(k + 1) * P], xkT[:, k * P:(k + 1) * P], wT[:, 2, :],
                                      start=True, stop=True)
            mm.then_inc(kv_ps, 1)

        @block.scalar
        def _(act):
            def take_y(b, part):
                act.wait_ge(y_turned, 2 * b + part + 1)
                nc.scalar.activation((yT_hi, yT_lo)[part][:, b * T:(b + 1) * T], f16(ps_x[:, BANK:2 * BANK]),
                                     ACT.Copy).then_inc(yT_ready, 1)

            def weigh(k, u):
                act.wait_ge(scores, k + 1)
                ge(act, split, k - RING + 1)
                nc.scalar.activation(e_f[:, u % RING, :], ps_s[:, u % 2, :], ACT.Exp,
                                     scale=1.0 / ROOT).then_inc(weights_f, 1)

            def round_hi(it, kl):
                u, m = kl % (2 * UNITS), (kl // 4) % 4
                if u not in ACT_SPLITS:
                    return
                act.wait_ge(weights_f, at(it, kl, 1) + 1)
                if kl % 4 == 0 or u - 1 not in ACT_SPLITS:
                    ge(act, product, 2 * at(it, kl, 4) - 6)
                j = kl % 4
                nc.scalar.activation(e_hi[:, m, 2 * j:2 * j + 2, :].rearrange("p s t -> p (s t)"),
                                     e_f[:, kl % RING, :], ACT.Copy).then_inc(rounded_a, 1)

            def pair(it, ffn):
                q, p = at_block(it), at_block(it) - 1
                for kk in range(2 * UNITS):
                    k, n, u, par = at(it, kk, 1), at(it, kk, UNITS), kk % UNITS, kk // UNITS
                    if live(k, SLOTS):
                        weigh(k, u)
                    if live(at(it, kk - 1, 1), SLOTS):
                        round_hi(it, kk - 1)
                    for part in range(2):
                        if u == (4, 7)[part] and live(k, SLOTS):
                            act.wait_ge(values, 2 * n + part + 1)
                            ge(act, product, 4 * n - 4)
                            nc.scalar.activation(val[:, par, part * 4:part * 4 + 4, 0:C],
                                                 ps_x[:, 0:BANK].rearrange("p (s c) -> p s c", c=C),
                                                 ACT.Copy).then_inc(val_hi, 1)
                    if isinstance(it, int) and it + 1 < B and kk in (8, 13):
                        take_y(it + 1, kk // 13)
                    if ffn and live(p, EARLY):
                        if kk == 5:
                            act.wait_ge(b_turned, p + 1)
                            act.wait_ge(b_prev, p + 1)
                            nc.scalar.activation(zTb[:, 1:1 + P], ps_x[:, BANK:BANK + P], ACT.Copy).then_inc(b_zT, 1)
                        if kk == 8:
                            act.wait_ge(b_proj, p + 1)
                            ge(act, b_gated, p)
                            ge(act, b_kv, p)
                            nc.scalar.activation(actb[:, 0, :], ps_x[:, BANK + P:BANK + 2 * P], ACT.Exp, scale=-1.0)
                            nc.scalar.activation(actb[:, 1, :], ps_x[:, BANK + 2 * P:BANK + 3 * P],
                                                 ACT.Relu).then_inc(b_act, 1)

            take_y(0, 0)
            take_y(0, 1)
            act.wait_ge(w_scale, 1)
            nc.scalar.activation(w_hi[:], w_raw[:].rearrange("p h c -> p (h c)"), ACT.Copy,
                                 scale=ws[:, 1:2]).then_inc(w_rounded, 1)
            run(act, pair)

            act.wait_ge(key_ps, 1)
            nc.scalar.activation(xkT, ps_s[:, 0, :], ACT.Relu).then_inc(key_relu, 1)
            act.wait_ge(gate_ps, 1)
            nc.scalar.activation(gate[:], ps_s[:, 1, :], ACT.Sigmoid).then_inc(gate_e, 1)

        @block.vector
        def _(dve):
            steps = [0]

            def step(ins):
                steps[0] += 1
                ins.then_inc(dve_step, 1)
                dve.wait_ge(dve_step, steps[0])

            def newton(y, ve, a, c, bits, rounds):
                step(dve.tensor_scalar(bits, ve.bitcast(I32), 1, None, ALU.logical_shift_right))
                step(dve.tensor_scalar(y.bitcast(I32), bits, -1.0, float(MAGIC), ALU.mult, ALU.add))
                for _ in range(rounds):
                    step(dve.scalar_tensor_tensor(out=a, in0=y, scalar=-0.5, in1=y, op0=ALU.mult, op1=ALU.mult))
                    step(dve.tensor_tensor(c, a, ve, ALU.mult))
                    step(dve.scalar_tensor_tensor(out=y, in0=c, scalar=1.5, in1=y, op0=ALU.add, op1=ALU.mult))

            def inv_root(var):
                ve, y, a, c = (nw[:, i, :] for i in range(4))
                step(dve.tensor_scalar(ve, var, EPS, None, ALU.add))
                newton(y, ve, a, c, nwi[:], 3)

            def layer_norm(dst, src):
                for k in range(NB):
                    i = dve.bn_stats(stats[:, k, :], src[:, k, :])
                step(i)
                for k in range(NB):
                    i = dve.bn_aggr(mv[:, k, :], stats[:, k, :])
                step(i)
                inv_root(mv[:, :, 1])
                for k in range(NB):
                    i = dve.tensor_scalar(dst[:, k, :], src[:, k, :], mv[:, k, 0:1], nw[:, 1, k:k + 1],
                                          ALU.subtract, ALU.mult)
                return i

            def weight_scale():
                dve.wait_ge(w_row, 1)
                step(dve.tensor_reduce(wmm[0:1, 0:1], ps_x[0:1, BANK:BANK + P], AX.X, ALU.max))
                step(dve.tensor_scalar(wmm[0:1, 1:2], wmm[0:1, 0:1], 1e-30, None, ALU.max))
                dve.tensor_scalar(ws[0:1, 0:1].bitcast(I32), wmm[0:1, 1:2].bitcast(I32), 0x7F800000, None,
                                  ALU.bitwise_and).then_inc(w_top, 1)
                dve.wait_ge(w_bc, 1)
                step(dve.tensor_copy(ws[:, 0:1], ps_x[:, BANK + P:BANK + P + 1]))
                dve.reciprocal(ws[:, 1:2], ws[:, 0:1]).then_inc(w_scale, 1)
                dve.wait_ge(w_rounded, 1)
                dve.scalar_tensor_tensor(out=w_lo[:], in0=w_raw[:].rearrange("p h c -> p (h c)"), scalar=ws[:, 1:2],
                                         in1=w_hi[:], op0=ALU.mult, op1=ALU.subtract).then_inc(w_ready, 1)
                dve.wait_ge(w_ready, 1)
                dve.wait_ge(f_turned, 1)
                dve.tensor_copy(wT[:].rearrange("p i c -> p (i c)"), ps_o[:, 0, 0:3 * P]).then_inc(f_ready, 1)

            def normalize_row(b):
                dve.wait_ge(x_in[b], 16)
                ge(dve, y_split, 2 * b)
                ge(dve, squared, b - 1)
                step(layer_norm(tmp, xs[:, b * NB:(b + 1) * NB, :]))

            def row_stats(b, blocks):
                dve.wait_ge(x_in[b], 16)
                for k in blocks:
                    dve.bn_stats(stats[:, k, :], xs[:, b * NB + k, :]).then_inc(row_summed, 1)

            def row_scale(b):
                dve.wait_ge(row_summed, NB * b)
                ge(dve, y_split, 2 * b)
                ge(dve, squared, b - 1)
                for k in range(NB):
                    i = dve.bn_aggr(mv[:, k, :], stats[:, k, :])
                step(i)
                inv_root(mv[:, :, 1])

            def row_apply(b):
                for k in range(NB):
                    i = dve.tensor_scalar(tmp[:, k, :], xs[:, b * NB + k, :], mv[:, k, 0:1], nw[:, 1, k:k + 1],
                                          ALU.subtract, ALU.mult)
                step(i)

            def split_row(b):
                hi, lo = y_hi[:, b * NB:(b + 1) * NB, :], y_lo[:, b * NB:(b + 1) * NB, :]
                dve.tensor_copy(hi, tmp[:]).then_inc(y_split, 1)
                if b == 0:
                    dve.wait_ge(y_split, 1)
                    dve.tensor_tensor(lo, tmp[:], hi, ALU.subtract).then_inc(y_split, 1)

            def row_squares(b):
                if b == 0:
                    step(dve.tensor_tensor(sq, tmp[:], tmp[:], ALU.mult))
                else:
                    dve.wait_ge(squared, b)
                step(dve.tensor_reduce(n2[:].rearrange("p h k -> p k h"),
                                       sq.rearrange("p k (h c) -> p k h c", c=HS), AX.X, ALU.add))
                dve.tensor_reduce(top2[:], n2[:], AX.X, ALU.max).then_inc(top_part, 1)

            def row_top(b):
                dve.wait_ge(top_row, b + 1)
                step(dve.tensor_reduce(tops[0:H, :], ps_x[0:H, BANK:BANK + P], AX.X, ALU.max))
                dve.tensor_scalar(diag[0:H, :], ident[0:H, 0:H], tops[0:H, 0:1], None, ALU.mult).then_inc(top_diag, 1)

            def row_bound(b):
                dve.wait_ge(top_bc, b + 1)
                dve.tensor_tensor(n2[:], n2[:], ps_x[:, BANK:BANK + H].unsqueeze(2).to_broadcast([P, H, NB]),
                                  ALU.mult).then_inc(bound2, 1)
                dve.wait_ge(bound2, b + 1)
                v = n2[:].rearrange("p h k -> p (h k)")
                y, a, c, bits = (gate[:, i * P:(i + 1) * P] for i in range(4))
                step(dve.tensor_scalar(v, v, 1e-30, None, ALU.max))
                newton(y, v, a, c, bits.bitcast(I32), 2)
                step(dve.scalar_tensor_tensor(out=a, in0=y, scalar=-1.0, in1=v, op0=ALU.mult, op1=ALU.mult))
                dve.tensor_scalar(shift[:, b * H:(b + 1) * H, :].rearrange("p h k -> p (h k)"), a,
                                  TOP * ROOT, None, ALU.add).then_inc(shift_ready, 1)
                dve.wait_ge(shift_ready, b + 1)

            def split_unit(it, kl):
                u, m, j = kl % (2 * UNITS), (kl // 4) % 4, kl % 4
                hi, lo = (e[:, m, 2 * j:2 * j + 2, :].rearrange("p s t -> p (s t)") for e in (e_hi, e_lo))
                ge(dve, product, 2 * at(it, kl, 4) - 6)
                if u in DVE_SPLITS:
                    dve.wait_ge(weights_f, at(it, kl, 1) + 1)
                    dve.tensor_copy(hi, e_f[:, kl % RING, :]).then_inc(rounded_v, 1)
                    dve.wait_ge(rounded_v, rounded(DVE_SPLITS, it, kl))
                else:
                    dve.wait_ge(rounded_a, rounded(ACT_SPLITS, it, kl))
                dve.tensor_tensor(lo, e_f[:, kl % RING, :], hi, ALU.subtract).then_inc(split, 1)

            def invert_sums(it, ql):
                bank, r = (ql // 2) % 2, at(it, ql, 2)
                dve.wait_ge(product, r + 1)
                ge(dve, added, r - 1)
                dve.reciprocal(rden[:, bank, :], ps_o[:, bank, C:C + BANK // 2 + 1:BANK // 2]).then_inc(den_ok, 1)

            def add_pair(it, ql):
                bank, r = (ql // 2) % 2, at(it, ql, 2)
                b = at(it, ql, UNITS) // H
                dve.wait_ge(den_ok, r + 1)
                ge(dve, added, r)
                for i in range(2):
                    dst = acc[:, bass.ds(b * NB + (ql - 1 + i) % 8, 1), :].rearrange("p a c -> p (a c)")
                    ins = dve.scalar_tensor_tensor(out=dst, in0=ps_o[:, bank, i * BANK // 2:i * BANK // 2 + C],
                                                   scalar=rden[:, bank, i:i + 1], in1=dst,
                                                   op0=ALU.mult, op1=ALU.add)
                ins.then_inc(added, 1)

            def pair(it, ffn):
                q, p = at_block(it), at_block(it) - 1
                for kk in range(2 * UNITS):
                    k, n, u, par = at(it, kk, 1), at(it, kk, UNITS), kk % UNITS, kk // UNITS
                    done = (kk - 5 - LAG) % 2 == 1 and live(at(it, kk - 5 - LAG, 1), BLOCKS)
                    if done:
                        invert_sums(it, kk - 5 - LAG)
                    if live(at(it, kk - 2, 1), SLOTS):
                        split_unit(it, kk - 2)
                    if done:
                        add_pair(it, kk - 5 - LAG)
                    if u == 5 and live(k, SLOTS):
                        split_values(n, par, 0)
                    if u == 0 and live(n - 1, NH):
                        split_values(n - 1, 1 - par, 1)
                    if u == 2 and live(k + UNITS, SLOTS):
                        take_operands(n + 1, 1 - par)
                    if isinstance(it, int) and it + 1 < B:
                        if kk < 4:
                            row_stats(it + 1, (2 * kk, 2 * kk + 1))
                        for at_slot, part in ((4, row_scale), (5, row_apply), (6, split_row), (9, row_squares),
                                              (11, row_top), (15, row_bound)):
                            if kk == at_slot:
                                part(it + 1)
                    if ffn and live(p, EARLY):
                        ffn_part(kk, p)
                    if ffn and live(q, EARLY):
                        norm_part(kk, q)

            def block_stats(i, q, src):
                ge(dve, root[i], ROOT_STEPS * q)
                dve.bn_stats(bst[:, i, :], src).then_inc(b_sum[i], 1)
                dve.wait_ge(b_sum[i], q + 1)
                dve.tensor_copy(idle[:], bst[:, i, :])
                dve.bn_aggr(bmv[:, i, :], bst[:, i, :]).then_inc(b_mean[i], 1)

            def norm_part(kk, q):
                if kk == 9:
                    ge(dve, b_x1, q)
                    dve.tensor_scalar(ab[:, 0, :], acc[:, bass.ds(q, 1), :].rearrange("p a c -> p (a c)"),
                                      ws[:, 0:1], None, ALU.mult).then_inc(b_scaled, 1)
                    dve.wait_ge(b_scaled, q + 1)
                    block_stats(0, q, ab[:, 0, :])
                if kk == 11:
                    dve.wait_ge(root[0], ROOT_STEPS * (q + 1))
                    dve.tensor_scalar(ab[:, 0, :], ab[:, 0, :], bmv[:, 0, 0:1], bnw[:, 0, 1:2],
                                      ALU.subtract, ALU.mult).then_inc(b_norm, 1)
                if kk == 13:
                    dve.wait_ge(b_x1, q + 1)
                    block_stats(1, q, ab[:, 1, :])
                if kk == 15:
                    dve.wait_ge(root[1], ROOT_STEPS * (q + 1))
                    ge(dve, b_turned, q)
                    dve.tensor_scalar(zb[:], ab[:, 1, :], bmv[:, 1, 0:1], bnw[:, 1, 1:2],
                                      ALU.subtract, ALU.mult).then_inc(b_z, 1)

            def ffn_part(kk, p):
                if kk == 6:
                    dve.wait_ge(b_zT, p + 1)
                    ge(dve, b_proj, p)
                    dve.tensor_tensor(mixb[:, 2, :], zTb[:, 1:1 + P], zTb[:, 0:P], ALU.subtract).then_inc(b_diff, 1)
                    dve.wait_ge(b_diff, p + 1)
                    for i in range(2):
                        ins = dve.scalar_tensor_tensor(out=mixb[:, i, :], in0=mixb[:, 2, :], scalar=mu[:, i:i + 1],
                                                       in1=zTb[:, 0:P], op0=ALU.mult, op1=ALU.add)
                    ins.then_inc(b_mixed, 1)
                if kk == 10:
                    dve.wait_ge(b_act1, p + 1)
                    dve.reciprocal(actb[:, 0, :], actb[:, 0, :]).then_inc(b_gate, 1)
                if kk == 14:
                    dve.wait_ge(b_kv, p + 1)
                    dve.wait_ge(b_gate, p + 1)
                    ge(dve, b_res, 2 * p)
                    dve.tensor_tensor(gb[:], actb[:, 0, :], ps_x[:, BANK + 3 * P:2 * BANK], ALU.mult).then_inc(b_gated, 1)
                    dve.wait_ge(b_gated, p + 1)
                    block_stats(2, p, gb[:])

            def split_values(n, par, part):
                dve.wait_ge(val_hi, 2 * n + part + 1)
                half = slice(part * 4, part * 4 + 4)
                dve.tensor_tensor(val[:, par, half, C + 1:VW], ps_x[:, 0:BANK].rearrange("p (s c) -> p s c", c=C),
                                  val[:, par, half, 0:C], ALU.subtract).then_inc(val_lo, 1)

            def take_operands(n, par):
                dve.wait_ge(turned, n + 1)
                ge(dve, scores, UNITS * (n - 1))
                dve.tensor_copy(op[:, par, :], f16(ps_x[:, 0:BANK])).then_inc(operands, 1)

            dve.memset(acc[:], 0.0).then_inc(zero_ok, 1)
            normalize_row(0)
            split_row(0)
            row_squares(0)
            dve.wait_ge(const_ok, 1)
            row_top(0)
            row_bound(0)
            dve.wait_ge(w_in, 16)
            dve.tensor_reduce(wmm[:, 0:1], w_raw[:], AX.XY, ALU.max)
            step(dve.tensor_reduce(wmm[:, 1:2], w_raw[:], AX.XY, ALU.min))
            dve.scalar_tensor_tensor(out=wmx[:, 0:1], in0=wmm[:, 1:2], scalar=-1.0, in1=wmm[:, 0:1],
                                     op0=ALU.mult, op1=ALU.max).then_inc(w_max, 1)
            take_operands(0, 0)
            weight_scale()
            dve.wait_ge(zero_ok, 1)
            run(dve, pair)

            dve.wait_ge(added, BLOCKS // 2)
            row = acc[:, EARLY:B * NB, :]
            flat = row.rearrange("p k c -> p (k c)")
            step(dve.tensor_scalar(flat, flat, ws[:, 0:1], None, ALU.mult))
            step(layer_norm(row, row))
            step(dve.tensor_tensor(row, row, xs[:, EARLY:B * NB, :], ALU.add))
            layer_norm(tmp, row).then_inc(z_ready, 1)
            dve.wait_ge(z_turned, 1)
            step(dve.tensor_copy(zT[:, 1:1 + T], ps_s[:, 0, :]))
            step(dve.tensor_tensor(xrT, zT[:, 1:1 + T], zT[:, 0:T], ALU.subtract))
            dve.scalar_tensor_tensor(out=xkT, in0=xrT, scalar=mu[:, 1:2], in1=zT[:, 0:T],
                                     op0=ALU.mult, op1=ALU.add).then_inc(mixed, 1)
            dve.wait_ge(mixed, 1)
            dve.scalar_tensor_tensor(out=xrT, in0=xrT, scalar=mu[:, 0:1], in1=zT[:, 0:T],
                                     op0=ALU.mult, op1=ALU.add).then_inc(mixed, 1)
            dve.wait_ge(key_relu, 1)
            dve.tensor_tensor(xkT, xkT, xkT, ALU.mult).then_inc(key_ok, 1)
            dve.wait_ge(gate_e, 1)
            dve.wait_ge(kv_ps, 1)
            g3 = gate[:].rearrange("p (k c) -> p k c", c=C)
            step(dve.tensor_tensor(gate[:], gate[:], ps_x[:], ALU.mult))
            step(layer_norm(tmp, g3))
            dve.tensor_tensor(tmp[:], tmp[:], row, ALU.add).then_inc(y_out, 1)


_INS = ['L0_attn_x', 'L0_attn_weight', 'L0_ffn_W_r', 'L0_ffn_W_k', 'L0_ffn_W_v', 'L0_ffn_mu_r', 'L0_ffn_mu_k']


def kernel(**inputs):
    import numpy as _np
    import concourse.bacc as _bacc
    from concourse import mybir as _mybir
    from concourse.bass_utils import run_bass_kernel_spmd as _run

    nc = _bacc.Bacc("TRN2", target_bir_lowering=False, num_devices=1)
    arrays, args = {}, []
    for name in _INS:
        a = _np.ascontiguousarray(inputs[name])
        arrays[f"in_{name}_dram"] = a
        args.append(nc.dram_tensor(f"in_{name}_dram", a.shape, _mybir.dt.from_np(a.dtype), kind="ExternalInput").ap())
    shape = _np.shape(inputs['L0_attn_x'])
    args.append(nc.dram_tensor("out_0_dram", shape, _mybir.dt.float32, kind="ExternalOutput").ap())
    sandwich(nc, *args)
    r = _run(nc, [arrays], core_ids=[0])
    return r.results[0]["out_0_dram"]
```

```python
from contextlib import ExitStack

import concourse.bass as bass
from concourse import mybir

F32 = mybir.dt.float32
F16 = mybir.dt.float16
I32 = mybir.dt.int32
ALU = mybir.AluOpType
ACT = mybir.ActivationFunctionType
AX = mybir.AxisListType

P = 128
BANK = 512
EPS = 1e-5

TOP = 10.5

LAG = 7
RING = 4
DVE_SPLITS = (5,)
MAGIC = 0x5F3759DF


def sandwich(nc, x, weight, w_r, w_k, w_v, mu_r, mu_k, out):
    B, T, C = x.shape
    H = weight.shape[0] // C
    HS = C // H
    NB = T // P
    NH = B * H
    UNITS = 8
    SLOTS = NH * UNITS
    BLOCKS = NH * NB
    assert C == P and NB == 8 and HS == 8 and T == 2 * BANK
    ROOT = float(HS) ** 0.5
    VW = 2 * C + 1

    ctx = ExitStack()
    with ctx:
        def sb(name, shape, dt):
            return ctx.enter_context(nc.sbuf_tensor(name, shape, dt))

        def sem(name):
            return ctx.enter_context(nc.semaphore(name))

        ps_s = ctx.enter_context(nc.psum_tensor("ps_s", [P, 2, 2 * BANK], F32))
        ps_o = ctx.enter_context(nc.psum_tensor("ps_o", [P, 2, BANK], F32))
        ps_x = ctx.enter_context(nc.psum_tensor("ps_x", [P, 2 * BANK], F32))

        ident = sb("ident", [P, P], F32)
        ident16 = sb("ident16", [P, P], F16)
        ones = sb("ones", [P, P], F32)
        xs = sb("xs", [P, B * NB, C], F32)
        w_raw = sb("w_raw", [P, H, C], F32)
        w_hi = sb("w_hi", [P, H * C], F16)
        w_lo = sb("w_lo", [P, H * C], F16)
        wf = sb("wf", [P, 3, C], F32)
        wT = sb("wT", [P, 3, C], F32)
        mu = sb("mu", [P, 2], F32)
        y_hi = sb("y_hi", [P, B * NB, C], F16)
        y_lo = sb("y_lo", [P, B * NB, C], F16)
        yT_hi = sb("yT_hi", [P, B * T], F16)
        yT_lo = sb("yT_lo", [P, B * T], F16)
        shift = sb("shift", [P, NH, NB], F16)
        acc = sb("acc", [P, B * NB, C], F32)
        st_stage = sb("st_stage", [P, 2, 4, 2, 2, 32], F16)
        mv_stage = sb("mv_stage", [P, 2, 4, 2, 2, 32], F16)
        op = sb("op", [P, 2, 8 * P], F16)
        e_f = sb("e_f", [P, RING, 2 * BANK], F32)
        e_hi = sb("e_hi", [P, 4, NB, BANK], F16)
        e_lo = sb("e_lo", [P, 4, NB, BANK], F16)
        val = sb("val", [P, 2, NB, VW], F16)
        rden = sb("rden", [P, 2, 2], F32)
        tmp = sb("tmp", [P, NB, C], F32)
        zT = sb("zT", [P, 1 + T], F32)
        xrT, xkT = (w_raw[:].rearrange("p h c -> p (h c)")[:, i * T:(i + 1) * T] for i in range(2))
        gate = sb("gate", [P, T], F32)
        sq = gate[:].rearrange("p (k c) -> p k c", c=C)
        keep = sb("keep", [P, B * NB], F32)
        zb = sb("zb", [P, C], F32)
        zTb = sb("zTb", [P, 1 + P], F32)
        mixb = sb("mixb", [P, 3, P], F32)
        actb = sb("actb", [P, 2, P], F32)
        gb = sb("gb", [P, C], F32)
        ob = sb("ob", [P, C], F32)
        bst = sb("bst", [P, 3, 6], F32)
        bmv = sb("bmv", [P, 3, 2], F32)
        bnw = sb("bnw", [P, 3, 4], F32)
        ab = sb("ab", [P, 2, C], F32)
        consts = sb("consts", [P, 3], F32)
        idle = sb("idle", [P, 6], F32)
        idle_act = sb("idle_act", [P, 1], F32)
        stats = sb("stats", [P, NB, 6], F32)
        mv = sb("mv", [P, NB, 2], F32)
        nw = sb("nw", [P, 4, NB], F32)
        nwi = sb("nwi", [P, NB], I32)
        away = sb("away", [P, NB], F32)
        n2 = sb("n2", [P, H, NB], F32)
        top2 = sb("top2", [P, H], F32)
        tops = sb("tops", [P, 1], F32)
        diag = sb("diag", [P, H], F32)
        wmm = sb("wmm", [P, 2], F32)
        wmx = sb("wmx", [P, 2], F32)
        ws = sb("ws", [P, 2], F32)
        ws2 = sb("ws2", [P, 1], F32)

        w_in, f_in = sem("w_in"), sem("f_in")
        x_in = [sem(f"x_in_{b}") for b in range(B)]
        const_ok, pool_zero = sem("const_ok"), sem("pool_zero")
        dve_step = sem("dve_step")
        w_scale, w_rounded, w_ready = sem("w_scale"), sem("w_rounded"), sem("w_ready")
        w_max, w_row, w_top, w_bc = sem("w_max"), sem("w_row"), sem("w_top"), sem("w_bc")
        f_turned = sem("f_turned")
        y_split, y_turned, yT_ready = sem("y_split"), sem("y_turned"), sem("yT_ready")
        top_part, top_row, top_diag, top_bc = sem("top_part"), sem("top_row"), sem("top_diag"), sem("top_bc")
        bound2, shift_ready, zero_ok = sem("bound2"), sem("shift_ready"), sem("zero_ok")
        squared, row_summed = sem("squared"), sem("row_summed")
        staged, turned, operands = sem("staged"), sem("turned"), sem("operands")
        scores, weights_f = sem("scores"), sem("weights_f")
        rounded_a, rounded_v, split = sem("rounded_a"), sem("rounded_v"), sem("split")
        values, val_hi, val_lo = sem("values"), sem("val_hi"), sem("val_lo")
        product, den_ok, added = sem("product"), sem("den_ok"), sem("added")
        z_ready, z_turned, zT_ready = sem("z_ready"), sem("z_turned"), sem("zT_ready")
        mixed = [sem(f"mixed_{g}") for g in range(2)]
        gate_ps, key_ps = sem("gate_ps"), sem("key_ps")
        gate_e, key_relu, key_ok, kv_ps = sem("gate_e"), sem("key_relu"), sem("key_ok"), sem("kv_ps")
        row_sum, row_mean, centred = sem("row_sum"), sem("row_mean"), sem("centred")
        kv_mean, kv_centred = sem("kv_mean"), sem("kv_centred")
        y_out, stored = [sem(f"y_out_{g}") for g in range(2)], sem("stored")
        root = [sem(f"root_{i}") for i in range(3)]
        ROOT_STEPS = 7
        b_sum = [sem(f"b_sum_{i}") for i in range(3)]
        b_mean = [sem(f"b_mean_{i}") for i in range(3)]
        b_scaled = sem("b_scaled")
        b_norm, b_x1, b_z, b_turned, b_prev = (sem(x) for x in ("b_norm", "b_x1", "b_z", "b_turned", "b_prev"))
        b_zT, b_diff, b_mixed, b_proj, b_act = (sem(x) for x in ("b_zT", "b_diff", "b_mixed", "b_proj", "b_act"))
        b_act1, b_gate, b_kv, b_gated = (sem(x) for x in ("b_act1", "b_gate", "b_kv", "b_gated"))
        b_res, b_out, b_stored = (sem(x) for x in ("b_res", "b_out", "b_stored"))

        x_v = x.rearrange("b (k p) c -> p b k c", p=P)
        out_v = out.rearrange("b (k p) c -> p b k c", p=P)
        out_b = out.rearrange("b (k p) c -> (b k) p c", p=P)
        EARLY = (B - 1) * NB
        PAIRS = NH // 2
        ROW = H // 2
        assert ROW == NB

        def f16(ap):
            return ap.bitcast(F16)

        def ge(eng, s, value):
            if isinstance(value, int) and value <= 0:
                return
            eng.wait_ge(s, value)

        def live(i, total):
            return not isinstance(i, int) or 0 <= i < total

        def at(it, kl, per):
            return 2 * UNITS // per * it + kl // per

        def heads_done(n):
            return min(n + 1, NH) if isinstance(n, int) else n + 1

        def at_block(it):
            return it - ROW

        def run(eng, pair):
            for it in range(B - 1):
                pair(it, False)
            with eng.Fori(B - 1, ROW) as it:
                pair(it, False)
            pair(ROW, True)
            with eng.Fori(ROW + 1, PAIRS - 1) as it:
                pair(it, True)
            pair(PAIRS - 1, True)
            pair(PAIRS, True)

        def blocks_of(g):
            return slice(g * NB // 2, (g + 1) * NB // 2)

        def tokens_of(g, shifted=0):
            return slice(g * BANK + shifted, (g + 1) * BANK + shifted)

        ACT_SPLITS = tuple(u for u in range(2 * UNITS) if u not in DVE_SPLITS)

        def rounded(group, it, kl):
            u = kl % (2 * UNITS)
            return at(it, kl, 2 * UNITS) * len(group) + sum(1 for g in group if g <= u)

        block = ctx.enter_context(nc.Block())

        @block.sync
        def _(sp):
            sp.dma_start(xs[:, 0:NB, :], x_v[:, 0]).then_inc(x_in[0], 16)
            sp.dma_start(w_raw[:], weight.rearrange("(h c) d -> c h d", c=C)).then_inc(w_in, 16)
            for i, w in enumerate((w_r, w_k, w_v)):
                sp.dma_start(wf[:, i, :], w).then_inc(f_in, 16)
            sp.dma_start(mu[:, 0:1], mu_r.rearrange("(c o) -> c o", o=1)).then_inc(f_in, 16)
            sp.dma_start(mu[:, 1:2], mu_k.rearrange("(c o) -> c o", o=1)).then_inc(f_in, 16)
            for b in range(1, B):
                sp.dma_start(xs[:, b * NB:(b + 1) * NB, :], x_v[:, b]).then_inc(x_in[b], 16)
            with sp.Fori(0, EARLY) as q:
                sp.wait_ge(b_out, q + 1)
                sp.dma_start(out_b[bass.ds(q, 1)].rearrange("q p c -> p (q c)"), ob[:]).then_inc(b_stored, 16)
            for g in range(2):
                sp.wait_ge(y_out[g], 1)
                sp.dma_start(out_v[:, B - 1, blocks_of(g)], tmp[:, blocks_of(g), :]).then_inc(stored, 16)
            sp.wait_ge(stored, 32)
            sp.wait_ge(b_stored, 16 * EARLY)

        @block.gpsimd
        def _(pool):
            nc.gpsimd.memset(ident[:], 0.0)
            nc.gpsimd.memset(mv_stage[:], 0.0)
            nc.gpsimd.memset(st_stage[:], 0.0)
            nc.gpsimd.memset(val[:, :, :, C:C + 1], 1.0)
            nc.gpsimd.memset(keep[:], 1.0)
            nc.gpsimd.memset(consts[:, 0:1], EPS)
            nc.gpsimd.memset(consts[:, 1:2], 1.5)
            nc.gpsimd.memset(consts[:, 2:3], -0.5)
            nc.gpsimd.memset(zTb[:], 0.0)
            nc.gpsimd.memset(zT[:, 0:1], 0.0)
            nc.gpsimd.memset(ones[:], 1.0).then_inc(pool_zero, 1)
            pool.wait_ge(pool_zero, 1)
            nc.gpsimd.memset(keep[:, 0:B * NB:NB], 0.0)
            nc.gpsimd.memset(st_stage[:, :, :, :, :, 3 * HS:3 * HS + 1], 1.0)
            nc.gpsimd.affine_select(out=ident[:], in_=ident[:], compare_op=ALU.not_equal, fill=1.0, base=0,
                                    pattern=[[-1, P]], channel_multiplier=1).then_inc(pool_zero, 1)
            pool.wait_ge(pool_zero, 2)
            nc.gpsimd.tensor_copy(ident16[:], ident[:]).then_inc(const_ok, 1)

            def stage(n, par):
                ge(pool, turned, n - 1)
                for a in range(2):
                    k0, c0 = n // H * NB + 4 * a, n % H * HS
                    hi, lo = (y[:, bass.ds(k0, 4), bass.ds(c0, HS)] for y in (y_hi, y_lo))
                    for d in range(2):
                        for i, part in enumerate((hi, hi, lo)):
                            nc.gpsimd.tensor_copy(st_stage[:, par, :, a, d, HS * i:HS * i + HS], part)
                        for i, part in enumerate((hi, lo, hi)):
                            nc.gpsimd.tensor_copy(mv_stage[:, par, :, d, a, HS * i:HS * i + HS], part)
                if isinstance(n, int) and n == 0:
                    pool.wait_ge(shift_ready, 1)
                for a in range(2):
                    for d in range(2):
                        last = nc.gpsimd.tensor_copy(mv_stage[:, par, :, d, a, 3 * HS:3 * HS + 1],
                                                     shift[:, n, 4 * a:4 * a + 4].unsqueeze(2))
                last.then_inc(staged, 1)

            def row_rest(b):
                pool.wait_ge(y_split, 2 * b + 1)
                nc.gpsimd.tensor_tensor(y_lo[:, b * NB:(b + 1) * NB, :], tmp[:], y_hi[:, b * NB:(b + 1) * NB, :],
                                        ALU.subtract).then_inc(y_split, 1)
                pool.wait_ge(shift_ready, b)
                nc.gpsimd.tensor_tensor(sq, tmp[:], tmp[:], ALU.mult).then_inc(squared, 1)

            def deviation(i, q):
                v, y, a = (bnw[:, i, c:c + 1] for c in range(3))
                done = [0]

                def step(out, in0, in1, op):
                    done[0] += 1
                    nc.gpsimd.tensor_tensor(out, in0, in1, op).then_inc(root[i], 1)
                    pool.wait_ge(root[i], q * ROOT_STEPS + done[0])

                pool.wait_ge(b_mean[i], q + 1)
                step(v, bmv[:, i, 1:2], consts[:, 0:1], ALU.add)
                step(y, v, consts[:, 2:3], ALU.pow)
                step(a, y, y, ALU.mult)
                step(a, a, v, ALU.mult)
                step(a, a, consts[:, 2:3], ALU.mult)
                step(a, a, consts[:, 1:2], ALU.add)
                step(y, y, a, ALU.mult)
                assert done[0] == ROOT_STEPS

            def pair(it, ffn):
                q, p = at_block(it), at_block(it) - 1
                if ffn and live(p, EARLY):
                    ge(pool, b_mixed, p)
                    nc.gpsimd.tensor_tensor(zTb[:, 0:1], zTb[:, P:P + 1], keep[:, bass.ds(p, 1)],
                                            ALU.mult).then_inc(b_prev, 1)
                if live(2 * it + 2, NH):
                    stage(2 * it + 2, 0)
                if live(2 * it + 3, NH):
                    stage(2 * it + 3, 1)
                if ffn and live(p, EARLY):
                    pool.wait_ge(b_act, p + 1)
                    nc.gpsimd.tensor_tensor(actb[:, 0, :], actb[:, 0, :], ones[:], ALU.add)
                    nc.gpsimd.tensor_tensor(actb[:, 1, :], actb[:, 1, :], actb[:, 1, :], ALU.mult).then_inc(b_act1, 1)
                if ffn and live(q, EARLY):
                    deviation(0, q)
                    pool.wait_ge(b_norm, q + 1)
                    rows, x_rows = (w[:, bass.ds(q, 1), :].rearrange("p a c -> p (a c)") for w in (acc, xs))
                    nc.gpsimd.tensor_tensor(rows, ab[:, 0, :], x_rows, ALU.add)
                    nc.gpsimd.tensor_tensor(ab[:, 1, :], ab[:, 0, :], x_rows, ALU.add).then_inc(b_x1, 1)
                    deviation(1, q)
                if ffn and live(p, EARLY):
                    deviation(2, p)
                    ge(pool, b_stored, 16 * p)
                    nc.gpsimd.tensor_tensor(ob[:], gb[:], bmv[:, 2, 0:1].to_broadcast([P, C]),
                                            ALU.subtract).then_inc(b_res, 1)
                    pool.wait_ge(b_res, 2 * p + 1)
                    nc.gpsimd.tensor_tensor(ob[:], ob[:], bnw[:, 2, 1:2].to_broadcast([P, C]),
                                            ALU.mult).then_inc(b_res, 1)
                    pool.wait_ge(b_res, 2 * p + 2)
                    nc.gpsimd.tensor_tensor(ob[:], ob[:], acc[:, bass.ds(p, 1), :].rearrange("p a c -> p (a c)"),
                                            ALU.add).then_inc(b_out, 1)
                if isinstance(it, int) and it + 1 < B:
                    row_rest(it + 1)
                    pool.wait_ge(shift_ready, it + 2)

            pool.wait_ge(y_split, 2)
            stage(0, 0)
            stage(1, 1)
            run(pool, pair)
            gated = gate[:].rearrange("p (k c) -> p k c", c=C)
            for g in range(2):
                pool.wait_ge(kv_mean, g + 1)
                nc.gpsimd.tensor_tensor(gated[:, blocks_of(g), :], gated[:, blocks_of(g), :],
                                        mv[:, blocks_of(g), 0:1].to_broadcast([P, NB // 2, C]),
                                        ALU.subtract).then_inc(kv_centred, 1)

        @block.tensor
        def _(pe):
            pe.wait_ge(const_ok, 1)
            aux = ps_x[:, BANK:2 * BANK]

            def weight_top():
                pe.wait_ge(w_max, 1)
                pe.wait_ge(yT_ready, 2)
                nc.tensor.transpose(aux[0:1, 0:P], wmx[:, 0:1], ident[:]).then_inc(w_row, 1)
                pe.wait_ge(w_top, 1)
                nc.tensor.matmul(aux[:, P:P + 1], ones[0:1, :], ws[0:1, 0:1], start=True, stop=True).then_inc(w_bc, 1)
                pe.wait_ge(f_in, 80)
                for i in range(3):
                    mm = nc.tensor.transpose(ps_o[:, 0, i * P:(i + 1) * P], wf[:, i, :], ident[:])
                mm.then_inc(f_turned, 1)

            def turn_y(b, part):
                pe.wait_ge(y_split, 2 * b + part + 1)
                ge(pe, bound2, b)
                for k in range(NB):
                    mm = nc.tensor.transpose(f16(aux)[:, k * P:(k + 1) * P],
                                             (y_hi, y_lo)[part][:, b * NB + k, :], ident16[:])
                mm.then_inc(y_turned, 1)

            def turn_top(b):
                pe.wait_ge(top_part, b + 1)
                pe.wait_ge(yT_ready, 2 * b + 1)
                nc.tensor.transpose(aux[0:H, 0:P], top2[:], ident[:]).then_inc(top_row, 1)

            def spread_top(b):
                pe.wait_ge(top_diag, b + 1)
                if b > 0:
                    pe.wait_ge(yT_ready, 2 * b + 2)
                nc.tensor.matmul(aux[:, 0:H], ones[0:H, :], diag[0:H, :], start=True, stop=True).then_inc(top_bc, 1)

            turn_y(0, 0)
            turn_top(0)
            spread_top(0)
            pe.wait_ge(bound2, 1)
            turn_y(0, 1)

            def turn_operands(n, par):
                pe.wait_ge(staged, n + 1)
                ge(pe, val_lo, 2 * n - 2)
                for j in range(4):
                    nc.tensor.transpose(f16(ps_x[:, 0:BANK])[:, j * P:(j + 1) * P],
                                        st_stage[:, par, j].rearrange("p a b k -> p (a b k)"), ident16[:])
                for j in range(4):
                    mm = nc.tensor.transpose(f16(ps_x[:, 0:BANK])[:, (4 + j) * P:(5 + j) * P],
                                             mv_stage[:, par, j].rearrange("p a b k -> p (a b k)"), ident16[:])
                mm.then_inc(turned, 1)

            def score_unit(k, u, par):
                half, j = u // 4, u % 4
                ge(pe, weights_f, k - 1)
                for a in range(2):
                    g = 32 * (2 * a + half)
                    mm = nc.tensor.matmul(ps_s[:, u % 2, a * BANK:(a + 1) * BANK],
                                          op[g:g + 32, par, j * P:(j + 1) * P],
                                          op[g:g + 32, par, 4 * P:8 * P], start=True, stop=True)
                mm.then_inc(scores, 1)

            def head_values(n, part):
                b, h = n // H, n % H
                if part == 0:
                    ge(pe, operands, heads_done(n + 1))
                else:
                    pe.wait_ge(val_lo, 2 * n + 1)
                for i in range(NB // 2):
                    pos = part * NB // 2 + i
                    j, a = pos // 2, pos % 2
                    t0 = b * T + (j + 4 * a) * P
                    dst = ps_x[:, i * C:(i + 1) * C]
                    nc.tensor.matmul(dst, yT_hi[:, bass.ds(t0, P)], w_hi[:, bass.ds(h * C, C)], start=True, stop=False)
                    nc.tensor.matmul(dst, yT_hi[:, bass.ds(t0, P)], w_lo[:, bass.ds(h * C, C)], start=False, stop=False)
                    mm = nc.tensor.matmul(dst, yT_lo[:, bass.ds(t0, P)], w_hi[:, bass.ds(h * C, C)], start=False, stop=True)
                mm.then_inc(values, 1)

            def products(it, ql):
                m, i = (ql // 4) % 4, ql % 4
                vp, bank, col = (ql // 8) % 2, (ql // 2) % 2, (ql % 2) * (BANK // 2)
                if i == 0:
                    pe.wait_ge(split, at(it, ql, 1) + 4)
                if ql % 8 == 0:
                    pe.wait_ge(val_lo, 2 * at(it, ql, 8) + 2)
                if ql % 2 == 0:
                    ge(pe, added, at(it, ql, 2) - 1)
                for s in range(NB):
                    hi, lo = (e[:, m, s, i * P:(i + 1) * P] for e in (e_hi, e_lo))
                    nc.tensor.matmul(ps_o[:, bank, col:col + C + 1], hi, val[:, vp, s, 0:C + 1],
                                     start=(s == 0), stop=False)
                    nc.tensor.matmul(ps_o[:, bank, col:col + C], hi, val[:, vp, s, C + 1:VW],
                                     start=False, stop=False)
                    mm = nc.tensor.matmul(ps_o[:, bank, col:col + C + 1], lo, val[:, vp, s, 0:C + 1],
                                          start=False, stop=(s == NB - 1))
                if ql % 2 == 1:
                    mm.then_inc(product, 1)

            def pair(it, ffn):
                q, p = at_block(it), at_block(it) - 1
                for kk in range(2 * UNITS):
                    k, n, u, par = at(it, kk, 1), at(it, kk, UNITS), kk % UNITS, kk // UNITS
                    if live(k, SLOTS):
                        if u == 0:
                            pe.wait_ge(operands, n + 1)
                        score_unit(k, u, par)
                    if live(at(it, kk - 4 - LAG, 1), BLOCKS):
                        products(it, kk - 4 - LAG)
                    if u == 1 and live(k + UNITS, SLOTS):
                        turn_operands(n + 1, 1 - par)
                    if u in (3, 6) and live(k, SLOTS):
                        if isinstance(it, int) and k == 3:
                            pe.wait_ge(w_ready, 1)
                        head_values(n, u // 6)
                    if isinstance(it, int) and it + 1 < B:
                        if kk == 7:
                            turn_y(it + 1, 0)
                        if kk == 10:
                            turn_top(it + 1)
                        if kk == 12:
                            pe.wait_ge(top_diag, it + 2)
                            turn_y(it + 1, 1)
                        if kk == 14:
                            spread_top(it + 1)
                    if ffn and live(p, EARLY):
                        if kk == 4:
                            pe.wait_ge(b_z, p + 1)
                            ge(pe, b_gated, p)
                            nc.tensor.transpose(aux[:, 0:P], zb[:], ident[:]).then_inc(b_turned, 1)
                        if kk == 7:
                            pe.wait_ge(b_mixed, p + 1)
                            nc.tensor.matmul(aux[:, P:2 * P], mixb[:, 0, :], wT[:, 0, :], start=True, stop=True)
                            nc.tensor.matmul(aux[:, 2 * P:3 * P], wT[:, 1, :], mixb[:, 1, :],
                                             start=True, stop=True).then_inc(b_proj, 1)
                        if kk == 12:
                            pe.wait_ge(b_act1, p + 1)
                            nc.tensor.matmul(aux[:, 3 * P:4 * P], actb[:, 1, :], wT[:, 2, :],
                                             start=True, stop=True).then_inc(b_kv, 1)

            turn_operands(0, 0)
            weight_top()
            run(pe, pair)

            def last_row_turn(g):
                pe.wait_ge(z_ready, g + 1)
                for k in range(NB)[blocks_of(g)]:
                    mm = nc.tensor.transpose(ps_s[:, 0, k * P:(k + 1) * P], tmp[:, k, :], ident[:])
                mm.then_inc(z_turned, 1)

            def last_row_keys(g):
                pe.wait_ge(mixed[g], 2)
                nc.tensor.matmul(ps_s[:, 0, tokens_of(g)], wT[:, 1, :], xkT[:, tokens_of(g)],
                                 start=True, stop=True).then_inc(key_ps, 1)

            def last_row_gate(g):
                pe.wait_ge(mixed[g], 3)
                for k in range(NB)[blocks_of(g)]:
                    mm = nc.tensor.matmul(ps_s[:, 1, k * P:(k + 1) * P], xrT[:, k * P:(k + 1) * P], wT[:, 0, :],
                                          start=True, stop=True)
                mm.then_inc(gate_ps, 1)

            def last_row_values(g):
                pe.wait_ge(key_ok, g + 1)
                if g == 0:
                    pe.wait_ge(val_lo, 2 * NH)
                else:
                    pe.wait_ge(b_gated, EARLY)
                for k in range(NB)[blocks_of(g)]:
                    mm = nc.tensor.matmul(ps_x[:, k * P:(k + 1) * P], xkT[:, k * P:(k + 1) * P], wT[:, 2, :],
                                          start=True, stop=True)
                mm.then_inc(kv_ps, 1)

            last_row_turn(0)
            last_row_turn(1)
            last_row_keys(0)
            last_row_gate(0)
            last_row_keys(1)
            last_row_values(0)
            last_row_gate(1)
            last_row_values(1)

        @block.scalar
        def _(act):
            def take_y(b, part):
                act.wait_ge(y_turned, 2 * b + part + 1)
                nc.scalar.activation((yT_hi, yT_lo)[part][:, b * T:(b + 1) * T], f16(ps_x[:, BANK:2 * BANK]),
                                     ACT.Copy).then_inc(yT_ready, 1)

            def weigh(k, u):
                act.wait_ge(scores, k + 1)
                ge(act, split, k - RING + 1)
                nc.scalar.activation(e_f[:, u % RING, :], ps_s[:, u % 2, :], ACT.Exp,
                                     scale=1.0 / ROOT).then_inc(weights_f, 1)

            def round_hi(it, kl):
                u, m = kl % (2 * UNITS), (kl // 4) % 4
                if u not in ACT_SPLITS:
                    return
                act.wait_ge(weights_f, at(it, kl, 1) + 1)
                if kl % 4 == 0 or u - 1 not in ACT_SPLITS:
                    ge(act, product, 2 * at(it, kl, 4) - 6)
                j = kl % 4
                nc.scalar.activation(e_hi[:, m, 2 * j:2 * j + 2, :].rearrange("p s t -> p (s t)"),
                                     e_f[:, kl % RING, :], ACT.Copy).then_inc(rounded_a, 1)

            def pair(it, ffn):
                q, p = at_block(it), at_block(it) - 1
                for kk in range(2 * UNITS):
                    k, n, u, par = at(it, kk, 1), at(it, kk, UNITS), kk % UNITS, kk // UNITS
                    if live(k, SLOTS):
                        weigh(k, u)
                    if live(at(it, kk - 1, 1), SLOTS):
                        round_hi(it, kk - 1)
                    for part in range(2):
                        if u == (4, 7)[part] and live(k, SLOTS):
                            act.wait_ge(values, 2 * n + part + 1)
                            ge(act, product, 4 * n - 4)
                            nc.scalar.activation(val[:, par, part * 4:part * 4 + 4, 0:C],
                                                 ps_x[:, 0:BANK].rearrange("p (s c) -> p s c", c=C),
                                                 ACT.Copy).then_inc(val_hi, 1)
                    if isinstance(it, int) and it + 1 < B and kk in (8, 13):
                        take_y(it + 1, kk // 13)
                    if ffn and live(p, EARLY):
                        if kk == 5:
                            act.wait_ge(b_turned, p + 1)
                            act.wait_ge(b_prev, p + 1)
                            nc.scalar.activation(zTb[:, 1:1 + P], ps_x[:, BANK:BANK + P], ACT.Copy).then_inc(b_zT, 1)
                        if kk == 8:
                            act.wait_ge(b_proj, p + 1)
                            ge(act, b_gated, p)
                            ge(act, b_kv, p)
                            nc.scalar.activation(actb[:, 0, :], ps_x[:, BANK + P:BANK + 2 * P], ACT.Exp, scale=-1.0)
                            nc.scalar.activation(actb[:, 1, :], ps_x[:, BANK + 2 * P:BANK + 3 * P],
                                                 ACT.Relu).then_inc(b_act, 1)

            take_y(0, 0)
            take_y(0, 1)
            act.wait_ge(w_scale, 1)
            nc.scalar.activation(w_hi[:], w_raw[:].rearrange("p h c -> p (h c)"), ACT.Copy,
                                 scale=ws[:, 1:2]).then_inc(w_rounded, 1)
            run(act, pair)

            act.wait_ge(row_mean, 1)
            for k in range(NB):
                rows = acc[:, EARLY + k, :]
                ins = nc.scalar.activation(rows, rows, ACT.Identity, bias=away[:, k:k + 1])
            ins.then_inc(centred, 1)
            nc.scalar.activation(idle_act[:], consts[:, 0:1], ACT.Sigmoid)
            for g in range(2):
                act.wait_ge(z_turned, g + 1)
                nc.scalar.activation(zT[:, tokens_of(g, 1)], ps_s[:, 0, tokens_of(g)], ACT.Copy).then_inc(zT_ready, 1)
            for g in range(2):
                here = tokens_of(g)
                act.wait_ge(key_ps, g + 1)
                nc.scalar.activation(xkT[:, here], ps_s[:, 0, here], ACT.Relu).then_inc(key_relu, 1)
                act.wait_ge(key_relu, g + 1)
                nc.scalar.activation(xkT[:, here], xkT[:, here], ACT.Square).then_inc(key_ok, 1)
                act.wait_ge(gate_ps, g + 1)
                nc.scalar.activation(gate[:, here], ps_s[:, 1, here], ACT.Sigmoid).then_inc(gate_e, 1)

        @block.vector
        def _(dve):
            steps = [0]

            def step(ins):
                steps[0] += 1
                ins.then_inc(dve_step, 1)
                dve.wait_ge(dve_step, steps[0])

            def newton(y, ve, a, c, bits, rounds):
                step(dve.tensor_scalar(bits, ve.bitcast(I32), 1, None, ALU.logical_shift_right))
                step(dve.tensor_scalar(y.bitcast(I32), bits, -1.0, float(MAGIC), ALU.mult, ALU.add))
                for _ in range(rounds):
                    step(dve.scalar_tensor_tensor(out=a, in0=y, scalar=-0.5, in1=y, op0=ALU.mult, op1=ALU.mult))
                    step(dve.tensor_tensor(c, a, ve, ALU.mult))
                    step(dve.scalar_tensor_tensor(out=y, in0=c, scalar=1.5, in1=y, op0=ALU.add, op1=ALU.mult))

            def inv_root(var, ks=slice(0, NB), scale2=1.0):
                ve, y, a, c = (nw[:, i, ks] for i in range(4))
                step(dve.tensor_scalar(ve, var, scale2, EPS, ALU.mult, ALU.add))
                newton(y, ve, a, c, nwi[:, ks], 3)

            def row_sums(src, ks):
                for k in range(NB)[ks]:
                    i = dve.bn_stats(stats[:, k, :], src[:, k, :])
                return i

            def row_moments(ks):
                for k in range(NB)[ks]:
                    i = dve.bn_aggr(mv[:, k, :], stats[:, k, :])
                return i

            def normalized(dst, src, ks):
                for k in range(NB)[ks]:
                    i = dve.tensor_scalar(dst[:, k, :], src[:, k, :], mv[:, k, 0:1], nw[:, 1, k:k + 1],
                                          ALU.subtract, ALU.mult)
                return i

            def scale_and_add(dst, src, residual, ks):
                for k in range(NB)[ks]:
                    i = dve.scalar_tensor_tensor(out=dst[:, k, :], in0=src[:, k, :], scalar=nw[:, 1, k:k + 1],
                                                 in1=residual[:, k, :], op0=ALU.mult, op1=ALU.add)
                return i

            def weight_scale():
                dve.wait_ge(w_row, 1)
                step(dve.tensor_reduce(wmm[0:1, 0:1], ps_x[0:1, BANK:BANK + P], AX.X, ALU.max))
                step(dve.tensor_scalar(wmm[0:1, 1:2], wmm[0:1, 0:1], 1e-30, None, ALU.max))
                dve.tensor_scalar(ws[0:1, 0:1].bitcast(I32), wmm[0:1, 1:2].bitcast(I32), 0x7F800000, None,
                                  ALU.bitwise_and).then_inc(w_top, 1)
                dve.wait_ge(w_bc, 1)
                step(dve.tensor_copy(ws[:, 0:1], ps_x[:, BANK + P:BANK + P + 1]))
                dve.reciprocal(ws[:, 1:2], ws[:, 0:1]).then_inc(w_scale, 1)
                dve.wait_ge(w_scale, 1)
                dve.tensor_tensor(ws2[:], ws[:, 0:1], ws[:, 0:1], ALU.mult)
                dve.wait_ge(w_rounded, 1)
                dve.scalar_tensor_tensor(out=w_lo[:], in0=w_raw[:].rearrange("p h c -> p (h c)"), scalar=ws[:, 1:2],
                                         in1=w_hi[:], op0=ALU.mult, op1=ALU.subtract).then_inc(w_ready, 1)
                dve.wait_ge(w_ready, 1)
                dve.wait_ge(f_turned, 1)
                dve.tensor_copy(wT[:].rearrange("p i c -> p (i c)"), ps_o[:, 0, 0:3 * P])

            def normalize_row(b):
                dve.wait_ge(x_in[b], 16)
                ge(dve, y_split, 2 * b)
                ge(dve, squared, b - 1)
                step(row_sums(xs[:, b * NB:(b + 1) * NB, :], slice(0, NB)))
                step(row_moments(slice(0, NB)))
                inv_root(mv[:, :, 1])
                step(normalized(tmp, xs[:, b * NB:(b + 1) * NB, :], slice(0, NB)))

            def row_stats(b, blocks):
                dve.wait_ge(x_in[b], 16)
                for k in blocks:
                    dve.bn_stats(stats[:, k, :], xs[:, b * NB + k, :]).then_inc(row_summed, 1)

            def row_scale(b):
                dve.wait_ge(row_summed, NB * b)
                ge(dve, y_split, 2 * b)
                ge(dve, squared, b - 1)
                step(row_moments(slice(0, NB)))
                inv_root(mv[:, :, 1])

            def row_apply(b):
                step(normalized(tmp, xs[:, b * NB:(b + 1) * NB, :], slice(0, NB)))

            def split_row(b):
                dve.tensor_copy(y_hi[:, b * NB:(b + 1) * NB, :], tmp[:]).then_inc(y_split, 1)

            def row_squares(b):
                if b == 0:
                    step(dve.tensor_tensor(sq, tmp[:], tmp[:], ALU.mult))
                else:
                    dve.wait_ge(squared, b)
                step(dve.tensor_reduce(n2[:].rearrange("p h k -> p k h"),
                                       sq.rearrange("p k (h c) -> p k h c", c=HS), AX.X, ALU.add))
                dve.tensor_reduce(top2[:], n2[:], AX.X, ALU.max).then_inc(top_part, 1)

            def row_top(b):
                dve.wait_ge(top_row, b + 1)
                step(dve.tensor_reduce(tops[0:H, :], ps_x[0:H, BANK:BANK + P], AX.X, ALU.max))
                dve.tensor_scalar(diag[0:H, :], ident[0:H, 0:H], tops[0:H, 0:1], None, ALU.mult).then_inc(top_diag, 1)

            def row_bound(b):
                dve.wait_ge(top_bc, b + 1)
                dve.tensor_tensor(n2[:], n2[:], ps_x[:, BANK:BANK + H].unsqueeze(2).to_broadcast([P, H, NB]),
                                  ALU.mult).then_inc(bound2, 1)
                dve.wait_ge(bound2, b + 1)
                v = n2[:].rearrange("p h k -> p (h k)")
                y, a, c, bits = (gate[:, i * P:(i + 1) * P] for i in range(4))
                step(dve.tensor_scalar(v, v, 1e-30, None, ALU.max))
                newton(y, v, a, c, bits.bitcast(I32), 2)
                step(dve.scalar_tensor_tensor(out=a, in0=y, scalar=-1.0, in1=v, op0=ALU.mult, op1=ALU.mult))
                dve.tensor_scalar(shift[:, b * H:(b + 1) * H, :].rearrange("p h k -> p (h k)"), a,
                                  TOP * ROOT, None, ALU.add).then_inc(shift_ready, 1)
                dve.wait_ge(shift_ready, b + 1)

            def split_unit(it, kl):
                u, m, j = kl % (2 * UNITS), (kl // 4) % 4, kl % 4
                hi, lo = (e[:, m, 2 * j:2 * j + 2, :].rearrange("p s t -> p (s t)") for e in (e_hi, e_lo))
                ge(dve, product, 2 * at(it, kl, 4) - 6)
                if u in DVE_SPLITS:
                    dve.wait_ge(weights_f, at(it, kl, 1) + 1)
                    dve.tensor_copy(hi, e_f[:, kl % RING, :]).then_inc(rounded_v, 1)
                    dve.wait_ge(rounded_v, rounded(DVE_SPLITS, it, kl))
                else:
                    dve.wait_ge(rounded_a, rounded(ACT_SPLITS, it, kl))
                dve.tensor_tensor(lo, e_f[:, kl % RING, :], hi, ALU.subtract).then_inc(split, 1)

            def invert_sums(it, ql):
                bank, r = (ql // 2) % 2, at(it, ql, 2)
                dve.wait_ge(product, r + 1)
                ge(dve, added, r - 1)
                dve.reciprocal(rden[:, bank, :], ps_o[:, bank, C:C + BANK // 2 + 1:BANK // 2]).then_inc(den_ok, 1)

            def add_pair(it, ql):
                bank, r = (ql // 2) % 2, at(it, ql, 2)
                b = at(it, ql, UNITS) // H
                dve.wait_ge(den_ok, r + 1)
                ge(dve, added, r)
                for i in range(2):
                    dst = acc[:, bass.ds(b * NB + (ql - 1 + i) % 8, 1), :].rearrange("p a c -> p (a c)")
                    ins = dve.scalar_tensor_tensor(out=dst, in0=ps_o[:, bank, i * BANK // 2:i * BANK // 2 + C],
                                                   scalar=rden[:, bank, i:i + 1], in1=dst,
                                                   op0=ALU.mult, op1=ALU.add)
                ins.then_inc(added, 1)

            def pair(it, ffn):
                q, p = at_block(it), at_block(it) - 1
                for kk in range(2 * UNITS):
                    k, n, u, par = at(it, kk, 1), at(it, kk, UNITS), kk % UNITS, kk // UNITS
                    done = (kk - 5 - LAG) % 2 == 1 and live(at(it, kk - 5 - LAG, 1), BLOCKS)
                    if done:
                        invert_sums(it, kk - 5 - LAG)
                    if live(at(it, kk - 2, 1), SLOTS):
                        split_unit(it, kk - 2)
                    if done:
                        add_pair(it, kk - 5 - LAG)
                        if isinstance(it, int):
                            for g in range(2):
                                if at(it, kk - 5 - LAG, 1) + 1 == BLOCKS - (1 - g) * NB // 2:
                                    last_row_sums(g)
                    if u == 5 and live(k, SLOTS):
                        split_values(n, par, 0)
                    if u == 0 and live(n - 1, NH):
                        split_values(n - 1, 1 - par, 1)
                    if u == 2 and live(k + UNITS, SLOTS):
                        take_operands(n + 1, 1 - par)
                    if isinstance(it, int) and it + 1 < B:
                        if kk < 4:
                            row_stats(it + 1, (2 * kk, 2 * kk + 1))
                        for at_slot, part in ((4, row_scale), (5, row_apply), (6, split_row), (9, row_squares),
                                              (11, row_top), (15, row_bound)):
                            if kk == at_slot:
                                part(it + 1)
                    if ffn and live(p, EARLY):
                        ffn_part(kk, p)
                    if ffn and live(q, EARLY):
                        norm_part(kk, q)

            last_row = acc[:, EARLY:B * NB, :]

            def last_row_sums(g):
                dve.wait_ge(added, BLOCKS // 2 - (1 - g) * NB // 4)
                row_sums(last_row, blocks_of(g)).then_inc(row_sum, 1)

            def last_row_norms():
                dve.wait_ge(row_sum, 2)
                step(row_moments(slice(0, NB)))
                dve.tensor_scalar(away[:], mv[:, :, 0], -1.0, None, ALU.mult).then_inc(row_mean, 1)
                inv_root(mv[:, :, 1], slice(0, NB), ws2[:])
                step(dve.tensor_scalar(nw[:, 1, :], nw[:, 1, :], ws[:, 0:1], None, ALU.mult))
                dve.wait_ge(centred, 1)
                step(scale_and_add(last_row, last_row, xs[:, EARLY:B * NB, :], slice(0, NB)))
                step(row_sums(last_row, slice(0, NB)))
                step(row_moments(slice(0, NB)))
                inv_root(mv[:, :, 1])
                for g in range(2):
                    normalized(tmp, last_row, blocks_of(g)).then_inc(z_ready, 1)

            def block_stats(i, q, src):
                ge(dve, root[i], ROOT_STEPS * q)
                dve.bn_stats(bst[:, i, :], src).then_inc(b_sum[i], 1)
                dve.wait_ge(b_sum[i], q + 1)
                dve.tensor_copy(idle[:], bst[:, i, :])
                dve.bn_aggr(bmv[:, i, :], bst[:, i, :]).then_inc(b_mean[i], 1)

            def norm_part(kk, q):
                if kk == 9:
                    ge(dve, b_x1, q)
                    dve.tensor_scalar(ab[:, 0, :], acc[:, bass.ds(q, 1), :].rearrange("p a c -> p (a c)"),
                                      ws[:, 0:1], None, ALU.mult).then_inc(b_scaled, 1)
                    dve.wait_ge(b_scaled, q + 1)
                    block_stats(0, q, ab[:, 0, :])
                if kk == 11:
                    dve.wait_ge(root[0], ROOT_STEPS * (q + 1))
                    dve.tensor_scalar(ab[:, 0, :], ab[:, 0, :], bmv[:, 0, 0:1], bnw[:, 0, 1:2],
                                      ALU.subtract, ALU.mult).then_inc(b_norm, 1)
                if kk == 13:
                    dve.wait_ge(b_x1, q + 1)
                    block_stats(1, q, ab[:, 1, :])
                if kk == 15:
                    dve.wait_ge(root[1], ROOT_STEPS * (q + 1))
                    ge(dve, b_turned, q)
                    dve.tensor_scalar(zb[:], ab[:, 1, :], bmv[:, 1, 0:1], bnw[:, 1, 1:2],
                                      ALU.subtract, ALU.mult).then_inc(b_z, 1)

            def ffn_part(kk, p):
                if kk == 6:
                    dve.wait_ge(b_zT, p + 1)
                    ge(dve, b_proj, p)
                    dve.tensor_tensor(mixb[:, 2, :], zTb[:, 1:1 + P], zTb[:, 0:P], ALU.subtract).then_inc(b_diff, 1)
                    dve.wait_ge(b_diff, p + 1)
                    for i in range(2):
                        ins = dve.scalar_tensor_tensor(out=mixb[:, i, :], in0=mixb[:, 2, :], scalar=mu[:, i:i + 1],
                                                       in1=zTb[:, 0:P], op0=ALU.mult, op1=ALU.add)
                    ins.then_inc(b_mixed, 1)
                if kk == 10:
                    dve.wait_ge(b_act1, p + 1)
                    dve.reciprocal(actb[:, 0, :], actb[:, 0, :]).then_inc(b_gate, 1)
                if kk == 14:
                    dve.wait_ge(b_kv, p + 1)
                    dve.wait_ge(b_gate, p + 1)
                    ge(dve, b_res, 2 * p)
                    dve.tensor_tensor(gb[:], actb[:, 0, :], ps_x[:, BANK + 3 * P:2 * BANK], ALU.mult).then_inc(b_gated, 1)
                    dve.wait_ge(b_gated, p + 1)
                    block_stats(2, p, gb[:])

            def split_values(n, par, part):
                dve.wait_ge(val_hi, 2 * n + part + 1)
                half = slice(part * 4, part * 4 + 4)
                dve.tensor_tensor(val[:, par, half, C + 1:VW], ps_x[:, 0:BANK].rearrange("p (s c) -> p s c", c=C),
                                  val[:, par, half, 0:C], ALU.subtract).then_inc(val_lo, 1)

            def take_operands(n, par):
                dve.wait_ge(turned, n + 1)
                ge(dve, scores, UNITS * (n - 1))
                dve.tensor_copy(op[:, par, :], f16(ps_x[:, 0:BANK])).then_inc(operands, 1)

            dve.memset(acc[:], 0.0).then_inc(zero_ok, 1)
            normalize_row(0)
            split_row(0)
            row_squares(0)
            dve.wait_ge(y_split, 1)
            dve.tensor_tensor(y_lo[:, 0:NB, :], tmp[:], y_hi[:, 0:NB, :], ALU.subtract).then_inc(y_split, 1)
            dve.wait_ge(w_in, 16)
            dve.tensor_reduce(wmm[:, 0:1], w_raw[:], AX.XY, ALU.max)
            dve.wait_ge(const_ok, 1)
            row_top(0)
            row_bound(0)
            step(dve.tensor_reduce(wmm[:, 1:2], w_raw[:], AX.XY, ALU.min))
            dve.scalar_tensor_tensor(out=wmx[:, 0:1], in0=wmm[:, 1:2], scalar=-1.0, in1=wmm[:, 0:1],
                                     op0=ALU.mult, op1=ALU.max).then_inc(w_max, 1)
            take_operands(0, 0)
            weight_scale()
            dve.wait_ge(zero_ok, 1)
            run(dve, pair)

            last_row_norms()
            for g in range(2):
                this, before = zT[:, tokens_of(g, 1)], zT[:, tokens_of(g)]
                xr, xk = xrT[:, tokens_of(g)], xkT[:, tokens_of(g)]
                dve.wait_ge(zT_ready, g + 1)
                dve.tensor_tensor(xr, this, before, ALU.subtract).then_inc(mixed[g], 1)
                dve.wait_ge(mixed[g], 1)
                dve.scalar_tensor_tensor(out=xk, in0=xr, scalar=mu[:, 1:2], in1=before,
                                         op0=ALU.mult, op1=ALU.add).then_inc(mixed[g], 1)
                dve.wait_ge(mixed[g], 2)
                dve.scalar_tensor_tensor(out=xr, in0=xr, scalar=mu[:, 0:1], in1=before,
                                         op0=ALU.mult, op1=ALU.add).then_inc(mixed[g], 1)
            gated = gate[:].rearrange("p (k c) -> p k c", c=C)
            for g in range(2):
                dve.wait_ge(gate_e, g + 1)
                dve.wait_ge(kv_ps, g + 1)
                step(dve.tensor_tensor(gate[:, tokens_of(g)], gate[:, tokens_of(g)], ps_x[:, tokens_of(g)], ALU.mult))
                step(row_sums(gated, blocks_of(g)))
                row_moments(blocks_of(g)).then_inc(kv_mean, 1)
            dve.wait_ge(kv_mean, 2)
            inv_root(mv[:, :, 1])
            for g in range(2):
                dve.wait_ge(kv_centred, g + 1)
                scale_and_add(tmp, gated, last_row, blocks_of(g)).then_inc(y_out[g], 1)


_INS = ['L0_attn_x', 'L0_attn_weight', 'L0_ffn_W_r', 'L0_ffn_W_k', 'L0_ffn_W_v', 'L0_ffn_mu_r', 'L0_ffn_mu_k']


def kernel(**inputs):
    import numpy as _np
    import concourse.bacc as _bacc
    from concourse import mybir as _mybir
    from concourse.bass_utils import run_bass_kernel_spmd as _run

    nc = _bacc.Bacc("TRN2", target_bir_lowering=False, num_devices=1)
    arrays, args = {}, []
    for name in _INS:
        a = _np.ascontiguousarray(inputs[name])
        arrays[f"in_{name}_dram"] = a
        args.append(nc.dram_tensor(f"in_{name}_dram", a.shape, _mybir.dt.from_np(a.dtype), kind="ExternalInput").ap())
    shape = _np.shape(inputs['L0_attn_x'])
    args.append(nc.dram_tensor("out_0_dram", shape, _mybir.dt.float32, kind="ExternalOutput").ap())
    sandwich(nc, *args)
    r = _run(nc, [arrays], core_ids=[0])
    return r.results[0]["out_0_dram"]
```
